# Optimizing a Trainium2 kernel written in Bass

```python
import numpy as np
import jax
import jax.numpy as jnp

def _softmax(x, axis=-1):
    return jax.nn.softmax(x, axis=axis)

def _gelu(x):
    return jax.nn.gelu(x, approximate=True)

def _silu(x):
    return jax.nn.silu(x)

def _sigmoid(x):
    return jax.nn.sigmoid(x)

def _layernorm(x, axis=-1, eps=1e-05):
    m = jnp.mean(x, axis=axis, keepdims=True)
    v = jnp.var(x, axis=axis, keepdims=True)
    return (x - m) / jnp.sqrt(v + eps)

def _scatter_add(tgt, idx, src, axis=0):
    return tgt.at[idx].add(src)

def _segment_sum(src, seg, n):
    return jax.ops.segment_sum(src, seg, n)
kernel_name = 'mk_gnn_resnorm_d1_gnn_r32_bc97b8'

def setup_inputs(seed: int=0):
    np.random.seed(seed)
    _w = jnp.asarray

    def _rec_inputs():
        import jax
        import jax.numpy as jnp
        _gk = jax.random.key(seed)
        x = -0.000202 + 1 * jax.random.normal(jax.random.fold_in(_gk, 1), (3125, 128), jnp.float32)
        _s = jax.random.randint(jax.random.fold_in(_gk, 2), (50000,), 0, 3125, jnp.int32)
        _d = jax.random.randint(jax.random.fold_in(_gk, 3), (50000,), 0, 3125, jnp.int32)
        _loop = jnp.arange(3125, dtype=jnp.int32)
        src = jnp.concatenate([_s, _d, _loop])
        dst = jnp.concatenate([_d, _s, _loop])
        _o = jnp.argsort(dst, stable=True)
        src = src[_o]
        dst = dst[_o]
        edge_attr_16 = -1.40915e-05 + 1.00011 * jax.random.normal(jax.random.fold_in(_gk, 12), (103125, 16), jnp.float32)
        return (x, src, dst, edge_attr_16)
    x, src, dst, edge_attr_16 = _rec_inputs()

    def _L0_gnn_setup():
        import jax, jax.numpy as jnp
        import numpy as np
        N_NODES = 50000
        N_EDGES = 20000
        HIDDEN = 128
        EDGE_FEATS = 16
        NUM_LAYERS = 4
        NUM_GRAPHS = 64
        LN_EPS = 1e-05
        key = jax.random.key(seed)
        ks = jax.random.split(key, 12)
        s = 1.0 / np.sqrt(HIDDEN)
        se = 1.0 / np.sqrt(EDGE_FEATS)
        return {'x': jax.random.normal(ks[0], (N_NODES, HIDDEN), jnp.float32), 'batch_index': jnp.sort(jax.random.randint(ks[1], (N_NODES,), 0, NUM_GRAPHS)), 'edge_index': jax.random.randint(ks[2], (2, N_EDGES), 0, N_NODES), 'edge_attr': jax.random.normal(ks[3], (N_EDGES, EDGE_FEATS), jnp.float32), 'We': jax.random.uniform(ks[4], (EDGE_FEATS, HIDDEN), jnp.float32, -se, se), 'be': jax.random.uniform(ks[5], (HIDDEN,), jnp.float32, -se, se), 'W1': jax.random.uniform(ks[6], (NUM_LAYERS, HIDDEN, HIDDEN), jnp.float32, -s, s), 'b1': jax.random.uniform(ks[7], (NUM_LAYERS, HIDDEN), jnp.float32, -s, s), 'W2': jax.random.uniform(ks[8], (NUM_LAYERS, HIDDEN, HIDDEN), jnp.float32, -s, s), 'b2': jax.random.uniform(ks[9], (NUM_LAYERS, HIDDEN), jnp.float32, -s, s), 'ln_g': jnp.ones((NUM_LAYERS, HIDDEN), jnp.float32), 'ln_b': jnp.zeros((NUM_LAYERS, HIDDEN), jnp.float32)}
    _L0_gnn_all = _L0_gnn_setup()
    _L0_gnn_in = {k: v for k, v in _L0_gnn_all.items() if k in ('We', 'be', 'W1', 'b1', 'W2', 'b2', 'ln_g', 'ln_b')}
    del _L0_gnn_all
    return {'x': x, 'src': src, 'dst': dst, 'edge_attr_16': edge_attr_16, 'L0_gnn_We': _L0_gnn_in['We'], 'L0_gnn_be': _L0_gnn_in['be'], 'L0_gnn_W1': _L0_gnn_in['W1'], 'L0_gnn_b1': _L0_gnn_in['b1'], 'L0_gnn_W2': _L0_gnn_in['W2'], 'L0_gnn_b2': _L0_gnn_in['b2'], 'L0_gnn_ln_g': _L0_gnn_in['ln_g'], 'L0_gnn_ln_b': _L0_gnn_in['ln_b']}

def reference(x, src, dst, edge_attr_16, L0_gnn_We, L0_gnn_be, L0_gnn_W1, L0_gnn_b1, L0_gnn_W2, L0_gnn_b2, L0_gnn_ln_g, L0_gnn_ln_b):
    import jax
    import jax.numpy as jnp

    def _L0_gnn_ref(x, batch_index, edge_index, edge_attr, We, be, W1, b1, W2, b2, ln_g, ln_b):
        import jax, jax.numpy as jnp
        import numpy as np
        N_NODES = 50000
        N_EDGES = 20000
        HIDDEN = 128
        EDGE_FEATS = 16
        NUM_LAYERS = 4
        NUM_GRAPHS = 64
        LN_EPS = 1e-05
        n = x.shape[0]
        src, dst = (edge_index[0], edge_index[1])
        ea = edge_attr @ We + be
        h = x
        for l in range(W1.shape[0]):
            m = jax.nn.relu(h[src] + ea)
            agg = jax.ops.segment_sum(m, dst, num_segments=n)
            z = h + agg
            z = jax.nn.relu(z @ W1[l] + b1[l]) @ W2[l] + b2[l]
            mu = jnp.mean(z, axis=-1, keepdims=True)
            var = jnp.var(z, axis=-1, keepdims=True)
            z = (z - mu) / jnp.sqrt(var + LN_EPS) * ln_g[l] + ln_b[l]
            h = jax.nn.relu(z) + h
        return h
    edge_index = jnp.stack([src, dst])
    batch0 = jnp.zeros((3125,), jnp.int32)
    x = _layernorm(x + _L0_gnn_ref(x, batch0, edge_index, edge_attr_16, L0_gnn_We, L0_gnn_be, L0_gnn_W1, L0_gnn_b1, L0_gnn_W2, L0_gnn_b2, L0_gnn_ln_g, L0_gnn_ln_b), axis=-1)
    return x

_drawn_inputs = setup_inputs


def setup_inputs(seed=0):
    import zlib

    import numpy as np

    out = dict(_drawn_inputs(seed))
    spreads = {'L0_gnn_ln_g': (1.0, 0.2), 'L0_gnn_ln_b': (0.0, 0.1)}
    factors = {'L0_gnn_b1': 8.0, 'L0_gnn_b2': 8.0}
    for name, (base, spread) in spreads.items():
        noise = np.random.default_rng([zlib.crc32(name.encode()), seed]).standard_normal(out[name].shape)
        drawn = base * np.exp(spread * noise) if base else spread * noise
        out[name] = jnp.asarray(drawn.astype(out[name].dtype))
    for name, factor in factors.items():
        out[name] = (out[name] * factor).astype(out[name].dtype)
    return out
```

```python
import concourse.bass as bass
from concourse import mybir
from contextlib import ExitStack

F32 = mybir.dt.float32
I32 = mybir.dt.int32
ALU = mybir.AluOpType
ACT = mybir.ActivationFunctionType
AX = mybir.AxisListType

NODES, HID = 3125, 128
EDGES, FEATS = 103125, 16
LAYERS = 4
EPS = 1e-5

P = 128
TPG = 7
GE = P * TPG
GROUPS = -(-EDGES // GE)
SLOTS = 4
STEPS = GROUPS // SLOTS
TAIL0 = EDGES - GE
OVERLAP = (GROUPS - 1) * GE - TAIL0
AW = TPG * FEATS
MW = TPG * HID
HALF = MW // 2

WIN = 64
WINDOWS = -(-NODES // WIN)
ZW = NODES + WIN
NOWHERE = -1.0e6

NB = 125
BPC = 5
CHUNKS = NODES // (NB * BPC)
CN = NB * BPC
CF = BPC * HID
CA, CB = 3 * NB, 2 * NB
assert SLOTS * STEPS == GROUPS and CHUNKS * CN == NODES


def gnn_kernel(nc, x, src, dst, attr, we, be, w1, b1, w2, b2, ln_g, ln_b, out):
    ctx = ExitStack()
    with ctx:
        def sb(name, shape, dt=F32):
            return ctx.enter_context(nc.sbuf_tensor(name, shape, dt))

        def ps(name, cols):
            return ctx.enter_context(nc.psum_tensor(name, [P, cols], F32))

        def sem(name):
            return ctx.enter_context(nc.semaphore(name))

        table = nc.dram_tensor("table", (NODES, HID), F32, kind="Internal").ap()

        attr_rows = sb("attr_rows", [P, GROUPS * AW])
        attr_cols = sb("attr_cols", [AW, GROUPS * P])
        src_rows = sb("src_rows", [GROUPS, GE], I32)
        dst_rows = sb("dst_rows", [GROUPS, GE], I32)
        src_f = sb("src_f", [GROUPS, GE])
        dst_f = sb("dst_f", [GROUPS, GE])
        off_f = sb("off_f", [GROUPS, GE])
        first = sb("first", [GROUPS, 1])
        reach = sb("reach", [GROUPS, 1])
        src_cols = sb("src_cols", [P, (GROUPS + SLOTS) * TPG], I32)
        dst_cols = sb("dst_cols", [P, GROUPS * TPG])
        off_cols = sb("off_cols", [P, GROUPS * TPG])
        first_row = sb("first_row", [1, GROUPS], I32)
        reach_row = sb("reach_row", [1, GROUPS])
        widest = sb("widest", [1, 1])
        widest_i = sb("widest_i", [1, 1], I32)

        ident = sb("ident", [P, P])
        node_i = sb("node_i", [P, WIN], I32)
        node_f = sb("node_f", [P, WIN])
        we_diag = sb("we_diag", [AW, MW])
        w12 = sb("w12", [P, LAYERS, 2 * HID])
        w_now = sb("w_now", [P, 2 * HID])
        b1_cols = sb("b1_cols", [P, LAYERS])
        b2_all = sb("b2_all", [NB, LAYERS * HID])
        g_all = sb("g_all", [NB, LAYERS * HID])
        b_all = sb("b_all", [NB, LAYERS * HID])
        be_all = sb("be_all", [NB, HID])
        eps = sb("eps", [NB, 1])

        x_rows = sb("x_rows", [NB, CHUNKS, CF])
        h_rows = sb("h_rows", [NB, CHUNKS, CF])
        tab_rows = sb("tab_rows", [NB, CHUNKS, CF])
        z_cols = sb("z_cols", [P, ZW])

        src_now = sb("src_now", [P, SLOTS, TPG], I32)
        gath = attr_rows[:, 0:SLOTS * MW].rearrange("p (s m) -> p s m", s=SLOTS)
        attr_now = sb("attr_now", [AW, P])
        msg = attr_rows[:, SLOTS * MW:(SLOTS + 1) * MW]
        hot = sb("hot", [P, TPG, WIN])
        dst_now = sb("dst_now", [P, TPG])
        hid = attr_rows[:, (SLOTS + 1) * MW:(SLOTS + 1) * MW + CN]
        spare = (SLOTS + 1) * MW + CN
        z2 = attr_rows[0:NB, spare:spare + CF]
        zn = attr_rows[0:NB, spare + CF:spare + 2 * CF]
        stats = sb("stats", [NB, BPC, 6])
        mv = sb("mv", [NB, BPC, 2])
        std = sb("std", [NB, BPC])
        rstd = sb("rstd", [NB, BPC])

        p_ea = ps("p_ea", 1024)
        p_win = ps("p_win", 512)
        p_z2 = ps("p_z2", 1024)
        p_tr = ps("p_tr", 1024)

        s_attr = [sem(f"attr_loaded{k}") for k in range(SLOTS)]
        s_ends = sem("ends_loaded")
        s_x = sem("x_loaded")
        s_par = sem("params_loaded")
        s_diag = sem("we_diag_loaded")
        s_const = sem("consts_made")
        s_masked = sem("overlap_masked")
        s_prep = sem("dve_prep")
        s_tr = sem("prep_transposed")
        s_trc = sem("prep_copied")
        s_atr = sem("attr_transposed")
        s_atc = sem("attr_copied")
        s_flag = sem("flag_ready")
        s_staged = [sem(f"indices_staged{s}") for s in range(SLOTS)]
        s_gath = [sem(f"rows_gathered{s}") for s in range(SLOTS)]
        s_attrnow = sem("attr_staged")
        s_ea = sem("edge_term_ready")
        s_pre = sem("sum_ready")
        s_msg = sem("message_ready")
        s_hot = sem("one_hot_ready")
        s_win = sem("window_ready")
        s_added = sem("window_added")
        s_tile = sem("targets_moved")
        s_wnow = sem("weights_staged")
        s_hidp = sem("hidden_summed")
        s_hid = sem("hidden_ready")
        s_z2p = sem("update_summed")
        s_z2 = sem("update_taken")
        s_dve = sem("dve_steps")
        s_var = sem("variance_ready")
        s_std = sem("deviation_ready")
        s_h = sem("h_ready")
        s_tab = sem("table_rows_ready")
        s_htr = sem("h_transposed")
        s_zc = sem("sums_started")
        s_table = sem("table_written")
        s_final = sem("final_rows_ready")
        s_out = sem("output_written")
        s_apart = sem("waits_done")

        x_view = x.rearrange("(c b p) f -> c p b f", p=NB, b=BPC)
        out_view = out.rearrange("(c b p) f -> c p b f", p=NB, b=BPC)
        table_view = table.rearrange("(c b p) f -> c p b f", p=NB, b=BPC)

        def blocks(ap):
            return ap.rearrange("p (b f) -> p b f", b=BPC)

        def by_layer(ap, l):
            return ap[:, bass.ds(l * HID, HID)].unsqueeze(1).to_broadcast((NB, BPC, HID))

        def apart(eng):
            eng.sem_inc(s_apart, 1)

        block = ctx.enter_context(nc.Block())

        @block.sync
        def _(sp):
            flat = lambda a: a.rearrange("(o n) -> o n", o=1)
            for rows, ends in ((dst_rows, dst), (src_rows, src)):
                sp.dma_start(rows[0:GROUPS - 1, :], ends[0:(GROUPS - 1) * GE].rearrange("(g n) -> g n", n=GE)).then_inc(s_ends, 16)
                sp.dma_start(rows[GROUPS - 1:GROUPS, :], flat(ends[TAIL0:EDGES])).then_inc(s_ends, 16)
            for c in range(CHUNKS):
                sp.dma_start(x_rows[:, c, :].rearrange("p (b f) -> p b f", b=BPC), x_view[c]).then_inc(s_x, 16)
            sp.dma_start(be_all[:, :], flat(be).to_broadcast((NB, HID))).then_inc(s_x, 16)
            for k in range(SLOTS):
                lo, hi = k * STEPS, min((k + 1) * STEPS, GROUPS - 1)
                sp.dma_start(attr_rows[:, lo * AW:hi * AW].rearrange("p (g a) -> p g a", a=AW),
                             attr[lo * GE:hi * GE, :].rearrange("(g p t) f -> p g (t f)", p=P, t=TPG)).then_inc(s_attr[k], 16)
            sp.dma_start(attr_rows[:, (GROUPS - 1) * AW:GROUPS * AW],
                         attr[TAIL0:EDGES, :].rearrange("(p t) f -> p (t f)", t=TPG)).then_inc(s_attr[SLOTS - 1], 16)
            sp.wait_ge(s_const, 4)
            for t in range(TPG):
                sp.dma_start(we_diag[t * FEATS:(t + 1) * FEATS, t * HID:(t + 1) * HID], we).then_inc(s_diag, 16)
            sp.dma_start(w12[:, :, 0:HID], w1.rearrange("l k n -> k l n")).then_inc(s_par, 16)
            sp.dma_start(w12[:, :, HID:2 * HID], w2.rearrange("l k n -> k l n")).then_inc(s_par, 16)
            with nc.allow_non_contiguous_dma(reason="512 biases, once"):
                sp.dma_start(b1_cols[:, :], b1.rearrange("l n -> n l")).then_inc(s_par, 16)
            for rows, par in ((b2_all, b2), (g_all, ln_g), (b_all, ln_b)):
                sp.dma_start(rows[:, :], par.rearrange("(o l) n -> o (l n)", o=1).to_broadcast((NB, LAYERS * HID))).then_inc(s_par, 16)
            for c in range(CHUNKS):
                sp.wait_ge(s_tab, c + 1)
                sp.dma_start(table_view[c], blocks(tab_rows[:, c, :])).then_inc(s_table, 16)
            with sp.Fori(0, LAYERS) as l:
                for c in range(CHUNKS):
                    sp.wait_ge(s_tab, (l + 1) * CHUNKS + c + 1)
                    sp.dma_start(table_view[c], blocks(tab_rows[:, c, :])).then_inc(s_table, 16)
            for c in range(CHUNKS):
                sp.wait_ge(s_final, c + 1)
                sp.dma_start(out_view[c], blocks(tab_rows[:, c, :])).then_inc(s_out, 16)
            sp.wait_ge(s_table, 16 * CHUNKS * (LAYERS + 1))
            sp.wait_ge(s_out, 16 * CHUNKS)

        @block.gpsimd
        def _(pool):
            nc.gpsimd.iota(node_i[:, :], pattern=[[1, WIN]], base=0, channel_multiplier=0).then_inc(s_const, 1)
            nc.gpsimd.memset(ident[:, :], 0.0).then_inc(s_const, 1)
            nc.gpsimd.memset(we_diag[:, :], 0.0).then_inc(s_const, 1)
            pool.wait_ge(s_const, 3)
            nc.gpsimd.affine_select(out=ident[:, :], in_=ident[:, :], compare_op=ALU.not_equal, fill=1.0,
                                    base=0, pattern=[[-1, P]], channel_multiplier=1).then_inc(s_const, 1)
            for n, rows in enumerate((dst_f, off_f)):
                pool.wait_ge(s_prep, 2 + 2 * n)
                nc.gpsimd.affine_select(out=rows[:, :], in_=rows[:, :], compare_op=ALU.is_ge, fill=NOWHERE,
                                        base=(GROUPS - 1) * GE - OVERLAP, pattern=[[1, GE]],
                                        channel_multiplier=-GE).then_inc(s_masked, 1)
            with pool.Fori(0, LAYERS) as l:
                pool.wait_ge(s_table, (l + 1) * (16 * CHUNKS))
                apart(pool)
                with pool.Fori(0, STEPS) as i:
                    for s in range(SLOTS):
                        pool.wait_ge(s_staged[s], l * STEPS + i + 1)
                        apart(pool)
                        for t in range(TPG):
                            nc.gpsimd.indirect_dma_start(
                                out=gath[:, s, t * HID:(t + 1) * HID], out_offset=None, in_=table,
                                in_offset=bass.IndirectOffsetOnAxis(ap=src_now[:, s, t:t + 1], axis=0),
                            ).then_inc(s_gath[s], 16)

        def stage_indices(g, s):
            nc.scalar.copy(src_now[:, s, :], src_cols[:, bass.ds(g * TPG, TPG)]).then_inc(s_staged[s], 1)

        def start_sums(act, c, h_count):
            act.wait_ge(s_htr, h_count)
            nc.scalar.copy(z_cols[:, c * CN:(c + 1) * CN].rearrange("p (b n) -> p b n", b=BPC),
                           blocks(p_tr[:, 0:CF])[:, :, 0:NB]).then_inc(s_zc, 1)

        @block.scalar
        def _(act):
            for g in range(GROUPS):
                act.wait_ge(s_atr, g + 1)
                bank = (p_ea[:, 0:P], p_ea[:, 512:512 + P])[g % 2]
                nc.scalar.copy(attr_cols[:, g * P:(g + 1) * P], bank[0:AW, :]).then_inc(s_atc, 1)
            for c in range(CHUNKS):
                start_sums(act, c, c + 1)
            act.wait_ge(s_trc, 2 * TPG + 2)
            for s in range(SLOTS):
                stage_indices(s, s)
            act.wait_ge(s_par, 16 * 6)
            with act.Fori(0, LAYERS) as l:
                nc.scalar.copy(w_now[:, :], w12[:, :, :].rearrange("p l n -> p (l n)")[:, bass.ds(l * (2 * HID), 2 * HID)]).then_inc(s_wnow, 1)
                with act.Fori(0, STEPS) as i:
                    for s in range(SLOTS):
                        g = i * SLOTS + s
                        n = l * GROUPS + g + 1
                        nc.scalar.copy(attr_now[:, :], attr_cols[:, bass.ds(g * P, P)]).then_inc(s_attrnow, 1)
                        act.wait_ge(s_pre, n)
                        nc.scalar.activation(msg[:, :], msg[:, :], ACT.Relu).then_inc(s_msg, 1)
                        stage_indices(g + SLOTS, s)
                n = l * CHUNKS
                for c in range(CHUNKS + 1):
                    if c < CHUNKS:
                        act.wait_ge(s_hidp, n + c + 1)
                        if c:
                            act.wait_ge(s_z2p, n + c)
                        apart(act)
                        bias = b1_cols[:, bass.ds(l, 1)]
                        nc.scalar.activation(hid[:, 0:CA], p_ea[:, 0:CA], ACT.Relu, bias=bias)
                        nc.scalar.activation(hid[:, CA:CN], p_ea[:, 512:512 + CB], ACT.Relu, bias=bias).then_inc(s_hid, 1)
                        act.wait_ge(s_var, n + c + 1)
                        nc.scalar.activation(std[:, :], mv[:, :, 1], ACT.Sqrt, bias=eps[:, 0:1]).then_inc(s_std, 1)
                    if c:
                        start_sums(act, c - 1, n + CHUNKS + c)
            for c in range(CHUNKS):
                act.wait_ge(s_var, LAYERS * CHUNKS + c + 1)
                nc.scalar.activation(std[:, :], mv[:, :, 1], ACT.Sqrt, bias=eps[:, 0:1]).then_inc(s_std, 1)

        @block.vector
        def _(dve):
            V = nc.vector
            V.memset(eps[:, :], EPS)
            V.memset(z_cols[:, NODES:ZW], 0.0)
            dve.wait_ge(s_const, 4)
            V.tensor_copy(node_f[:, :], node_i[:, :])
            dve.wait_ge(s_ends, 64)
            V.tensor_copy(src_f[:, :], src_rows[:, :]).then_inc(s_prep, 1)
            V.tensor_copy(dst_f[:, :], dst_rows[:, :]).then_inc(s_prep, 1)
            dve.wait_ge(s_masked, 1)
            V.tensor_copy(off_f[:, :], dst_rows[:, :]).then_inc(s_prep, 1)
            dve.wait_ge(s_prep, 3)
            V.tensor_reduce(first[:, :], off_f[:, :], axis=AX.X, op=ALU.min).then_inc(s_dve, 1)
            dve.wait_ge(s_dve, 1)
            V.tensor_scalar(off_f[:, :], off_f[:, :], first[:, 0:1], None, ALU.subtract).then_inc(s_prep, 1)
            dve.wait_ge(s_masked, 2)
            V.tensor_reduce(reach[:, :], off_f[:, :], axis=AX.X, op=ALU.max).then_inc(s_prep, 1)
            cols = lambda ap, t: ap.rearrange("p (g t) -> p g t", t=TPG)[:, :, t]
            for t in range(TPG):
                dve.wait_ge(s_tr, t + 1)
                for k, to in enumerate((src_cols[:, 0:GROUPS * TPG], dst_cols[:, :], off_cols[:, :])):
                    last = V.tensor_copy(cols(to, t), p_z2[:, k * P:k * P + GROUPS])
                last.then_inc(s_trc, 1)
            dve.wait_ge(s_trc, TPG)
            V.tensor_copy(src_cols[:, GROUPS * TPG:(GROUPS + SLOTS) * TPG], src_cols[:, 0:SLOTS * TPG]).then_inc(s_trc, TPG + 1)
            dve.wait_ge(s_tr, TPG + 1)
            V.tensor_copy(first_row[:, :], p_z2[0:1, 0:GROUPS])
            V.tensor_reduce(widest[:, :], p_z2[0:1, P:P + GROUPS], axis=AX.X, op=ALU.max).then_inc(s_dve, 1)
            dve.wait_ge(s_dve, 2)
            V.tensor_copy(widest_i[:, :], widest[:, :]).then_inc(s_trc, 1)
            for c in range(CHUNKS):
                dve.wait_ge(s_x, 16 * (CHUNKS + 1))
                V.tensor_copy(h_rows[:, c, :], x_rows[:, c, :])
                V.tensor_tensor(out=blocks(tab_rows[:, c, :]), in0=blocks(x_rows[:, c, :]),
                                in1=be_all[:, :].unsqueeze(1).to_broadcast((NB, BPC, HID)), op=ALU.add).then_inc(s_tab, 1)
            dve.wait_ge(s_trc, 2 * TPG + 2)
            wide = dve.value_load(widest_i[0:1, 0:1])

            done = [2, 0]

            def link(ins, base):
                done[1] += 1
                ins.then_inc(s_dve, 1)
                dve.wait_ge(s_dve, base + done[1])
                apart(dve)

            def normalize(base, count):
                for b in range(BPC):
                    last = V.bn_stats(stats[:, b, :], z2[:, b * HID:(b + 1) * HID])
                link(last, base)
                for b in range(BPC):
                    last = V.bn_aggr(mv[:, b, :], stats[:, b, :])
                last.then_inc(s_var, 1)
                dve.wait_ge(s_std, count)
                link(V.reciprocal(rstd[:, :], std[:, :]), base)
                for b in range(BPC):
                    last = V.tensor_scalar(zn[:, b * HID:(b + 1) * HID], z2[:, b * HID:(b + 1) * HID],
                                           mv[:, b, 0:1], rstd[:, b:b + 1], ALU.subtract, ALU.mult)
                return last

            with dve.Fori(0, LAYERS) as l:
                def group(n, s, use, node, windows):
                    dve.wait_ge(s_gath[s], use * (16 * TPG))
                    dve.wait_ge(s_ea, n + 1)
                    V.tensor_tensor(out=msg[:, :].rearrange("p (a m) -> p a m", a=2),
                                    in0=gath[:, s, :].rearrange("p (a m) -> p a m", a=2),
                                    in1=p_ea[:, :].rearrange("p (a m) -> p a m", a=2)[:, :, 0:HALF],
                                    op=ALU.add).then_inc(s_pre, 1)

                def one_hot(targets):
                    V.tensor_tensor(out=hot[:, :, :], in0=node_f[:, :].unsqueeze(1).to_broadcast((P, TPG, WIN)),
                                    in1=targets.unsqueeze(2).to_broadcast((P, TPG, WIN)),
                                    op=ALU.is_equal).then_inc(s_hot, 1)

                def add_window(at, count):
                    dve.wait_ge(s_win, count)
                    V.tensor_tensor(out=z_cols[:, bass.ds(at, WIN)], in0=z_cols[:, bass.ds(at, WIN)],
                                    in1=p_win[:, 0:WIN], op=ALU.add).then_inc(s_added, 1)

                dve.wait_ge(s_zc, (l + 1) * CHUNKS)
                apart(dve)
                with dve.If(wide < WIN):
                    with dve.Fori(0, STEPS) as i:
                        for s in range(SLOTS):
                            g = i * SLOTS + s
                            n = l * GROUPS + g
                            node = dve.value_load(first_row[0:1, bass.ds(g, 1)], min_val=0, max_val=NODES - 1)
                            one_hot(off_cols[:, bass.ds(g * TPG, TPG)])
                            group(n, s, l * STEPS + i + 1, node, 1)
                            add_window(node, n + 1)
                with dve.Else():
                    with dve.Fori(0, STEPS) as i:
                        for s in range(SLOTS):
                            g = i * SLOTS + s
                            n = l * GROUPS + g
                            V.tensor_copy(dst_now[:, :], dst_cols[:, bass.ds(g * TPG, TPG)]).then_inc(s_tile, 1)
                            group(n, s, l * STEPS + i + 1, None, WINDOWS)
                            with dve.Fori(0, WINDOWS) as w:
                                dve.wait_ge(s_tile, n * (WINDOWS + 1) + w + 1)
                                one_hot(dst_now[:, :])
                                add_window(w * WIN, n * WINDOWS + w + 1)
                                V.tensor_scalar(dst_now[:, :], dst_now[:, :], -float(WIN), None, ALU.add).then_inc(s_tile, 1)

                per_chunk = 5
                for c in range(CHUNKS):
                    done[1] = 0
                    base = l * (CHUNKS * per_chunk) + (done[0] + c * per_chunk)
                    n = l * CHUNKS + c
                    dve.wait_ge(s_z2p, n + 1)
                    z2_in = V.tensor_tensor(out=blocks(z2[:, :]), in0=blocks(p_z2[0:NB, 0:CF]), in1=by_layer(b2_all, l), op=ALU.add)
                    z2_in.then_inc(s_z2, 1)
                    dve.wait_ge(s_z2, n + 1)
                    link(normalize(base, n + 1), base)
                    link(V.tensor_tensor(out=blocks(zn[:, :]), in0=blocks(zn[:, :]), in1=by_layer(g_all, l), op=ALU.mult), base)
                    link(V.tensor_tensor(out=blocks(zn[:, :]), in0=blocks(zn[:, :]), in1=by_layer(b_all, l), op=ALU.add), base)
                    V.scalar_tensor_tensor(out=h_rows[:, c, :], in0=zn[:, :], scalar=0.0, in1=h_rows[:, c, :],
                                           op0=ALU.max, op1=ALU.add).then_inc(s_h, 1)
                    dve.wait_ge(s_h, n + 1)
                    V.tensor_tensor(out=blocks(tab_rows[:, c, :]), in0=blocks(h_rows[:, c, :]),
                                    in1=be_all[:, :].unsqueeze(1).to_broadcast((NB, BPC, HID)), op=ALU.add).then_inc(s_tab, 1)
                    assert done[1] == per_chunk
            base = done[0] + LAYERS * CHUNKS * per_chunk
            done[1] = 0
            dve.wait_ge(s_table, 16 * CHUNKS * (LAYERS + 1))
            for c in range(CHUNKS):
                link(V.tensor_tensor(out=z2[:, :], in0=x_rows[:, c, :], in1=h_rows[:, c, :], op=ALU.add), base)
                last = normalize(base, LAYERS * CHUNKS + c + 1)
                link(last, base)
                V.tensor_copy(tab_rows[:, c, :], zn[:, :]).then_inc(s_final, 1)

        @block.tensor
        def _(pe):
            T = nc.tensor

            def transpose_h(rows):
                for b in range(BPC):
                    last = T.transpose(p_tr[:, b * HID:b * HID + NB], rows[:, b * HID:(b + 1) * HID], ident[0:NB, 0:NB])
                last.then_inc(s_htr, 1)

            pe.wait_ge(s_const, 4)
            pe.wait_ge(s_prep, 5)
            cols = lambda ap, t: ap.rearrange("p (g t) -> p g t", t=TPG)[:, :, t]
            for t in range(TPG):
                if t:
                    pe.wait_ge(s_trc, t)
                for k, rows in enumerate((src_f, dst_f, off_f)):
                    last = T.transpose(p_z2[:, k * P:k * P + GROUPS], rows[:, :].rearrange("g (p t) -> g p t", t=TPG)[:, :, t],
                                       ident[0:GROUPS, 0:GROUPS])
                last.then_inc(s_tr, 1)
            pe.wait_ge(s_trc, 2 * TPG + 1)
            T.transpose(p_z2[0:1, 0:GROUPS], first[:, :], ident[0:GROUPS, 0:GROUPS])
            T.transpose(p_z2[0:1, P:P + GROUPS], reach[:, :], ident[0:GROUPS, 0:GROUPS]).then_inc(s_tr, 1)
            for g in range(GROUPS):
                k = min(g // STEPS, SLOTS - 1)
                if g % STEPS == 0:
                    pe.wait_ge(s_attr[k], 32 if k == SLOTS - 1 else 16)
                if g >= 2:
                    pe.wait_ge(s_atc, g - 1)
                bank = (p_ea[:, 0:P], p_ea[:, 512:512 + P])[g % 2]
                T.transpose(bank[0:AW, :], attr_rows[:, g * AW:(g + 1) * AW], ident[:, :]).then_inc(s_atr, 1)
            pe.wait_ge(s_x, 16 * (CHUNKS + 1))
            for c in range(CHUNKS):
                if c:
                    pe.wait_ge(s_zc, c)
                transpose_h(x_rows[:, c, :])
            pe.wait_ge(s_diag, 16 * TPG)
            pe.wait_ge(s_trc, 2 * TPG + 2)
            pe.wait_ge(s_atc, GROUPS)
            wide = pe.value_load(widest_i[0:1, 0:1])

            with pe.Fori(0, LAYERS) as l:
                def edge_term(n):
                    pe.wait_ge(s_attrnow, n + 1)
                    for a in range(2):
                        last = T.matmul(p_ea[:, a * 512:a * 512 + HALF], attr_now[:, :], we_diag[:, a * HALF:(a + 1) * HALF],
                                        start=True, stop=True)
                    last.then_inc(s_ea, 1)

                def sum_window():
                    for t in range(TPG):
                        last = T.matmul(p_win[:, 0:WIN], msg[:, t * HID:(t + 1) * HID], hot[:, t, :],
                                        start=(t == 0), stop=(t == TPG - 1))
                    last.then_inc(s_win, 1)

                with pe.If(wide < WIN):
                    with pe.Fori(0, GROUPS) as g:
                        n = l * GROUPS + g
                        edge_term(n)
                        pe.wait_ge(s_hot, n + 1)
                        pe.wait_ge(s_msg, n + 1)
                        sum_window()
                with pe.Else():
                    with pe.Fori(0, GROUPS) as g:
                        n = l * GROUPS + g
                        edge_term(n)
                        pe.wait_ge(s_msg, n + 1)
                        apart(pe)
                        with pe.Fori(0, WINDOWS) as w:
                            pe.wait_ge(s_hot, n * WINDOWS + w + 1)
                            sum_window()

                def hidden(c):
                    T.matmul(p_ea[:, 0:CA], w_now[:, 0:HID], z_cols[:, c * CN:c * CN + CA], start=True, stop=True)
                    T.matmul(p_ea[:, 512:512 + CB], w_now[:, 0:HID], z_cols[:, c * CN + CA:(c + 1) * CN],
                             start=True, stop=True).then_inc(s_hidp, 1)

                pe.wait_ge(s_wnow, l + 1)
                with pe.If(wide < WIN):
                    pe.wait_ge(s_added, (l + 1) * GROUPS)
                with pe.Else():
                    pe.wait_ge(s_added, (l + 1) * (GROUPS * WINDOWS))
                n = l * CHUNKS
                hidden(0)
                for c in range(CHUNKS):
                    pe.wait_ge(s_hid, n + c + 1)
                    if c:
                        pe.wait_ge(s_z2, n + c)
                    for b in range(BPC):
                        last = T.matmul(p_z2[0:NB, b * HID:(b + 1) * HID], hid[:, b * NB:(b + 1) * NB], w_now[:, HID:2 * HID],
                                        start=True, stop=True)
                    last.then_inc(s_z2p, 1)
                    if c + 1 < CHUNKS:
                        hidden(c + 1)
                    pe.wait_ge(s_h, n + c + 1)
                    pe.wait_ge(s_zc, n + CHUNKS + c)
                    transpose_h(h_rows[:, c, :])


_INS = ["x", "src", "dst", "edge_attr_16", "L0_gnn_We", "L0_gnn_be", "L0_gnn_W1", "L0_gnn_b1", "L0_gnn_W2", "L0_gnn_b2",
        "L0_gnn_ln_g", "L0_gnn_ln_b"]


def kernel(**inputs):
    import numpy as _np
    import concourse.bacc as _bacc
    from concourse import mybir as _mybir
    from concourse.bass_utils import run_bass_kernel_spmd as _run

    nc = _bacc.Bacc("TRN2", target_bir_lowering=False, num_devices=1)
    arrays, args = {}, []
    for name in _INS:
        a = _np.ascontiguousarray(inputs[name])
        arrays[f"in_{name}"] = a
        args.append(nc.dram_tensor(f"in_{name}", a.shape, _mybir.dt.from_np(a.dtype), kind="ExternalInput").ap())
    args.append(nc.dram_tensor("out", (NODES, HID), F32, kind="ExternalOutput").ap())
    gnn_kernel(nc, *args)
    r = _run(nc, [arrays], core_ids=[0])
    return r.results[0]["out"]
```

```python
import concourse.bass as bass
from concourse import mybir
from contextlib import ExitStack

F32 = mybir.dt.float32
BF16 = mybir.dt.bfloat16
FP8 = mybir.dt.float8e4
U8 = mybir.dt.uint8
I32 = mybir.dt.int32
ALU = mybir.AluOpType
ACT = mybir.ActivationFunctionType
AX = mybir.AxisListType

NODES, HID = 3125, 128
EDGES, FEATS = 103125, 16
LAYERS = 4
EPS = 1e-5
P = 128

NB = 125
BLOCKS = NODES // NB
BPG = 5
GROUPS = BLOCKS // BPG
GN = NB * BPG
GF = BPG * HID
GA, GB = 3 * NB, 2 * NB

EPP = 29
CE = P * EPP
CHUNKS = -(-EDGES // CE)
TAIL0 = EDGES - CE
OVERLAP = (CHUNKS - 1) * CE - TAIL0
SPARE = 5
TILES = BLOCKS + SPARE
SLOTS = P * TILES
ROWS = SLOTS + CE
REC = 20
TB = 4
BATCHES = -(-TILES // TB)
ACT_BATCHES = BLOCKS // TB
RING = 4
WIN = 128
ZW = NODES + WIN
WINDOWS = -(-NODES // WIN)
PAIRS = CHUNKS // 2
STACK = 6 * FEATS
NO_BLOCK, NOWHERE = 31.0, -1.0e6
DESCS = 16
assert CHUNKS == 2 * PAIRS and GROUPS * BPG == BLOCKS and BLOCKS == ACT_BATCHES * TB + 1


class Chain:

    def __init__(self, eng, sem):
        self.eng, self.sem, self.base, self.n = eng, sem, 0, 0

    def at(self, base):
        self.base, self.n = base, 0

    def __call__(self, ins):
        self.n += 1
        ins.then_inc(self.sem, 1)
        self.eng.wait_ge(self.sem, self.base + self.n)


def gnn_kernel(nc, x, src, dst, attr, we, be, w1, b1, w2, b2, ln_g, ln_b, out):
    ctx = ExitStack()
    with ctx:
        def sb(name, shape, dt=F32):
            return ctx.enter_context(nc.sbuf_tensor(name, shape, dt))

        def sem(name):
            return ctx.enter_context(nc.semaphore(name))

        table = nc.dram_tensor("table", (NODES, HID), F32, kind="Internal").ap()
        records = nc.dram_tensor("records", (CHUNKS * ROWS, REC), F32, kind="Internal").ap()
        stacks = nc.dram_tensor("stacks", (CHUNKS, STACK, SLOTS), BF16, kind="Internal").ap()
        picks = nc.dram_tensor("picks", (CHUNKS, NB, BLOCKS * P), U8, kind="Internal").ap()

        ident = sb("ident", [P, P])
        ident_b = sb("ident_b", [P, P], BF16)
        ones = sb("ones", [P, P])
        before = sb("before", [P, P], BF16)
        before_f = sb("before_f", [P, P])
        iota_i = sb("iota_i", [P, P], I32)
        iota_f = sb("iota_f", [P, P])
        part_i = sb("part_i", [P, 1], I32)
        part_f = sb("part_f", [P, 1])
        part1 = sb("part1", [P, 1])
        iota1 = sb("iota1", [P, WIN])
        steps_f = sb("steps_f", [P, SPARE - 1])
        lost_i = sb("lost_i", [P, EPP], I32)
        lost_f = sb("lost_f", [P, EPP])
        base_f = sb("base_f", [P, CHUNKS * EPP])
        we_f = sb("we_f", [FEATS, HID])
        we_rows = sb("we_rows", [STACK, 4, HID])
        we_stack = sb("we_stack", [STACK, HID], BF16)
        part_sel = sb("part_sel", [STACK, 4])
        w12 = sb("w12", [P, LAYERS * 2 * HID])
        w_now = sb("w_now", [P, 2 * HID])
        b1_cols = sb("b1_cols", [P, LAYERS])
        b2_row = sb("b2_row", [1, LAYERS * HID])
        g_all = sb("g_all", [NB, LAYERS * HID])
        b_all = sb("b_all", [NB, LAYERS * HID])
        be_all = sb("be_all", [NB, HID])
        be_wide = sb("be_wide", [NB, GF])
        eps = sb("eps", [NB, 1])
        zeros = sb("zeros", [P, TILES * REC])

        EC = CHUNKS * EPP
        src_i = sb("src_i", [P, EC], I32)
        dst_i = sb("dst_i", [P, EC], I32)
        block_f = sb("block_f", [P, EC])
        dst_f = sb("dst_f", [P, EC])
        tmp_a = sb("tmp_a", [P, EC])
        tmp_b = sb("tmp_b", [P, EC])
        tmp_i = sb("tmp_i", [P, EC], I32)
        base_i = tmp_i[:, :].rearrange("p (k t) -> p k t", t=EPP)
        meta = sb("meta", [P, EC, 4])
        ends = sb("ends", [P, 2, CHUNKS])
        span = sb("span", [CHUNKS, 4])
        first_row = sb("first_row", [1, 2 * CHUNKS])
        first_i = sb("first_i", [1, CHUNKS], I32)
        first_all = sb("first_all", [P, CHUNKS])
        own = sb("own", [P, EPP, BLOCKS], BF16)
        run = [sb(f"run{n}", [P, 16 + EPP, BLOCKS], BF16) for n in range(2)]
        rank_w = sb("rank_w", [P, EPP, BLOCKS])
        rank1 = sb("rank1", [P, EPP])
        over = sb("over", [P, EPP])
        orun = [sb(f"orun{n}", [P, 16 + EPP]) for n in range(2)]
        otot = sb("otot", [P, 1], BF16)
        rr = sb("rr", [P, EPP])
        steps_w = sb("steps_w", [P, EPP, SPARE - 1])
        up = sb("up", [P, EPP])
        tile_f = sb("tile_f", [P, EPP])
        row_f = sb("row_f", [P, EPP])
        bad_f = sb("bad_f", [P, EPP])
        most = sb("most", [P, EPP])
        most1 = sb("most1", [P, 1])
        flag_f = sb("flag_f", [1, 2])
        flag_i = sb("flag_i", [1, 1], I32)
        row_i = [sb(f"row_i{n}", [P, EPP], I32) for n in range(2)]
        rec = [sb(f"rec{n}", [P, EPP, REC]) for n in range(2)]
        slots = sb("slots", [P, TILES, REC])
        stack_rows = sb("stack_rows", [P, TILES, STACK], BF16)
        a_left = sb("a_left", [P, TILES, FEATS])
        local_b = sb("local_b", [P, BLOCKS], BF16)
        targets = sb("targets", [P, CHUNKS * TILES])
        spare_src = sb("spare_src", [P, (CHUNKS + 1) * SPARE], I32)

        stack_now = [sb(f"stack_now{n}", [STACK, SLOTS], BF16) for n in range(2)]
        pick_now = [sb(f"pick_now{n}", [NB, BLOCKS * P], FP8) for n in range(2)]
        spare_now = [sb(f"spare_now{n}", [P, SPARE], I32) for n in range(2)]
        gath = [sb(f"gath{n}", [P, SPARE * HID]) for n in range(2)]
        msg = [sb(f"msg{n}", [P, TB * HID]) for n in range(RING)]
        hot = [sb(f"hot{n}", [P, TB, WIN]) for n in range(RING)]

        x_rows = sb("x_rows", [NB, GROUPS, GF])
        h_rows = sb("h_rows", [NB, GROUPS, GF])
        tab_rows = sb("tab_rows", [NB, GROUPS, GF])
        parts = sb("parts", [NB, 3, GROUPS * GF], BF16)
        z_cols = sb("z_cols", [P, ZW])
        after_ranks = meta[:, :, :].rearrange("p e w -> p (e w)")
        rest = [after_ranks[0:NB, n * GF:(n + 1) * GF] for n in range(2)]
        hid = after_ranks[:, 2 * GF:2 * GF + GN]
        z2 = tmp_a[0:NB, 0:GF]
        zn = tmp_b[0:NB, 0:GF]
        stats = sb("stats", [NB, BPG, 6])
        mv = sb("mv", [NB, BPG, 2])
        std = sb("std", [NB, BPG])
        rstd = sb("rstd", [NB, BPG])

        g_attr = rec[0][:, :, :].rearrange("p t w -> p (t w)")[:, 0:EPP * FEATS]
        g_src = sb("g_src", [P, 1], I32)
        g_dst = sb("g_dst", [P, 1])
        g_feat = sb("g_feat", [P, FEATS])
        g_cols = sb("g_cols", [FEATS, P])
        g_rows = gath[0][:, 0:HID]
        g_msg = msg[0][:, 0:HID]
        g_hot = hot[0][:, 0, :]

        psum = ctx.enter_context(nc.psum_tensor("psum", [P, 8 * 512], F32))
        bank = lambda n, m=1: psum[:, n * 512:(n + m) * 512]
        p_hid, p_z2, p_tr = bank(0, 2), [bank(2, 2), bank(4, 2)], bank(6, 2)
        p_win = [bank(4), bank(5)]

        s_const = sem("consts_made")
        s_zero = sem("zeros_made")
        s_ends = sem("ends_loaded")
        s_x = sem("x_loaded")
        s_we = sem("we_loaded")
        s_par = sem("params_loaded")
        s_cleared = sem("records_cleared")
        s_prep = sem("prep_steps")
        s_prep_pe = sem("prep_products")
        s_masked = sem("overlap_masked")
        s_attr = [sem(f"attr_loaded{n}") for n in range(2)]
        s_rank = sem("rank_steps")
        s_tot = sem("totals_ready")
        s_pre = sem("totals_before")
        s_row = sem("rows_ready")
        s_scat = [sem(f"records_scattered{n}") for n in range(2)]
        s_slot = sem("slots_loaded")
        s_slotfree = sem("slots_used")
        s_unp = sem("unpack_steps")
        s_stackrows = sem("stack_rows_ready")
        s_local = sem("locals_ready")
        s_bc = sem("locals_spread")
        s_pick = sem("picks_ready")
        s_strp = sem("stack_transposed")
        s_stc = sem("stack_copied")
        s_saved = sem("chunk_saved")
        s_savefree = sem("save_place_free")
        s_flag = sem("flag_ready")

        s_str = [sem(f"stream_loaded{n}") for n in range(2)]
        s_staged = [sem(f"spare_staged{n}") for n in range(2)]
        s_gath = [sem(f"rows_gathered{n}") for n in range(2)]
        s_sum = sem("sums_ready")
        s_act = sem("messages_ready")
        s_left = sem("spare_messages_ready")
        s_leftstep = sem("spare_sums_ready")
        s_hot = sem("one_hot_ready")
        s_sc = sem("batch_scattered")
        s_added = sem("window_added")
        s_start = sem("edge_stage_starts")

        s_wnow = sem("weights_staged")
        s_hidp = sem("hidden_summed")
        s_hid = sem("hidden_ready")
        s_z2p = sem("update_summed")
        s_z2 = sem("update_taken")
        s_upd = sem("update_steps")
        s_var = sem("variance_ready")
        s_std = sem("deviation_ready")
        s_h = sem("h_ready")
        s_tab = sem("table_rows_ready")
        s_parts = sem("parts_ready")
        s_part1 = sem("part_1_ready")
        s_part2 = sem("part_2_ready")
        s_rest = sem("rest_ready")
        s_htr = sem("h_transposed")
        s_zc = sem("sums_started")
        s_table = sem("table_written")
        s_final = sem("final_rows_ready")
        s_out = sem("output_written")
        s_apart = sem("waits_done")

        s_gtrh = sem("general_h_transposed")
        s_gz = sem("general_sums_started")
        s_gattr = sem("general_attr")
        s_gfree = sem("general_attr_used")
        s_gtile = sem("general_tile")
        s_gtr = sem("general_transposed")
        s_gcols = sem("general_cols")
        s_gterm = sem("general_term")
        s_ggath = sem("general_gathered")
        s_gmsg = sem("general_message")
        s_ghot = sem("general_one_hot")
        s_gwin = sem("general_window")
        s_gadd = sem("general_added")
        s_gstep = sem("general_steps")

        x_view = x.rearrange("(c b p) f -> c p b f", p=NB, b=BPG)
        out_view = out.rearrange("(c b p) f -> c p b f", p=NB, b=BPG)
        table_view = table.rearrange("(c b p) f -> c p b f", p=NB, b=BPG)
        rec_view = records.rearrange("(k r) w -> k r w", r=ROWS)

        def blocks(ap):
            return ap.rearrange("p (b f) -> p b f", b=BPG)

        def apart(eng):
            eng.sem_inc(s_apart, 1)

        def flat(a):
            return a.rearrange("(o n) -> o n", o=1)

        def attr_of(k):
            if isinstance(k, int) and k == CHUNKS - 1:
                a = attr[TAIL0:EDGES, :]
            else:
                a = attr[bass.ds(k * CE, CE), :]
            return a.rearrange("(p t) f -> p t f", t=EPP)

        blk = ctx.enter_context(nc.Block())

        @blk.sync
        def _(sp):
            for rows, e in ((dst_i, dst), (src_i, src)):
                last = (CHUNKS - 1) * EPP
                sp.dma_start(rows[:, 0:last].rearrange("p (k t) -> p k t", t=EPP),
                             e[0:(CHUNKS - 1) * CE].rearrange("(k p t) -> p k t", p=P, t=EPP)).then_inc(s_ends, 16)
                sp.dma_start(rows[:, last:EC], e[TAIL0:EDGES].rearrange("(p t) -> p t", t=EPP)).then_inc(s_ends, 16)
            for n in range(2):
                sp.dma_start(rec[n][:, :, 0:FEATS], attr_of(n)).then_inc(s_attr[n], 16)
            for c in range(GROUPS):
                sp.dma_start(blocks(x_rows[:, c, :]), x_view[c]).then_inc(s_x, 16)
            sp.dma_start(be_all[:, :], flat(be).to_broadcast((NB, HID))).then_inc(s_x, 16)
            sp.dma_start(we_f[:, :], we).then_inc(s_we, 16)
            for n in range(STACK // FEATS):
                sp.dma_start(we_rows[n * FEATS:(n + 1) * FEATS, 0, :], we).then_inc(s_we, 16)
            sp.wait_ge(s_zero, 1)
            sp.dma_start(rec_view[:, 0:SLOTS, :].rearrange("k (p j) w -> p k (j w)", p=P),
                         zeros[:, :].unsqueeze(1).to_broadcast((P, CHUNKS, TILES * REC))).then_inc(s_cleared, 16)
            sp.dma_start(w12[:, :].rearrange("p (l n) -> p l n", l=LAYERS)[:, :, 0:HID], w1.rearrange("l k n -> k l n")).then_inc(s_par, 16)
            sp.dma_start(w12[:, :].rearrange("p (l n) -> p l n", l=LAYERS)[:, :, HID:2 * HID], w2.rearrange("l k n -> k l n")).then_inc(s_par, 16)
            with nc.allow_non_contiguous_dma(reason="512 biases, once"):
                sp.dma_start(b1_cols[:, :], b1.rearrange("l n -> n l")).then_inc(s_par, 16)
            sp.dma_start(b2_row[:, :], b2.rearrange("(o l) n -> o (l n)", o=1)).then_inc(s_par, 16)
            for rows, par in ((g_all, ln_g), (b_all, ln_b)):
                sp.dma_start(rows[:, :], par.rearrange("(o l) n -> o (l n)", o=1).to_broadcast((NB, LAYERS * HID))).then_inc(s_par, 16)

            def store_table(first):
                for c in range(GROUPS):
                    sp.wait_ge(s_tab, first + c + 1)
                    sp.dma_start(table_view[c], blocks(tab_rows[:, c, :])).then_inc(s_table, 16)

            store_table(0)

            def read_slots(k, s, use):
                sp.wait_ge(s_slotfree, k + 1)
                sp.wait_ge(s_scat[s], use * (16 * EPP))
                sp.dma_start(slots[:, :, :].rearrange("p j w -> p (j w)"),
                             rec_view[bass.ds(k, 1), 0:SLOTS, :].rearrange("o (p j) w -> p (o j w)", p=P)).then_inc(s_slot, 16)

            with sp.Fori(0, PAIRS - 2) as i:
                for s in range(2):
                    read_slots(i * 2 + s, s, i + 1)
                    sp.dma_start(rec[s][:, :, 0:FEATS], attr_of(i * 2 + s + 2)).then_inc(s_attr[s], 16)
            for s in range(2):
                read_slots(CHUNKS - 4 + s, s, PAIRS - 1)
                sp.dma_start(rec[s][:, :, 0:FEATS], attr_of(CHUNKS - 2 + s)).then_inc(s_attr[s], 16)
            for s in range(2):
                read_slots(CHUNKS - 2 + s, s, PAIRS)

            sp.wait_ge(s_saved, 32 * CHUNKS)
            sp.wait_ge(s_flag, 1)
            flag = sp.value_load(flag_i[0:1, 0:1])
            with sp.Fori(0, LAYERS) as l:
                with sp.If(0 < flag):
                    with sp.Fori(0, CHUNKS - 1) as k:
                        sp.wait_ge(s_gfree, l * CHUNKS + k + 1)
                        sp.dma_start(g_attr.rearrange("p (t f) -> p t f", f=FEATS), attr_of(k)).then_inc(s_gattr, 16)
                    sp.wait_ge(s_gfree, (l + 1) * CHUNKS)
                    sp.dma_start(g_attr.rearrange("p (t f) -> p t f", f=FEATS), attr_of(CHUNKS - 1)).then_inc(s_gattr, 16)
                store_table((l + 1) * GROUPS)
                with sp.If(l < LAYERS - 1):
                    with sp.Fori(0, PAIRS) as i:
                        for s in range(2):
                            k = i * 2 + s
                            sp.wait_ge(s_sum, ((l + 1) * CHUNKS + k - 1) * BATCHES)
                            sp.dma_start(stack_now[s][:, :], stacks[bass.ds(k, 1)].rearrange("o a b -> (o a) b")).then_inc(s_str[s], 16)
                            sp.dma_start(pick_now[s][:, :].bitcast(U8), picks[bass.ds(k, 1)].rearrange("o a b -> (o a) b")).then_inc(s_str[s], 16)
            for c in range(GROUPS):
                sp.wait_ge(s_final, c + 1)
                sp.dma_start(out_view[c], blocks(x_rows[:, c, :])).then_inc(s_out, 16)
            sp.wait_ge(s_table, 16 * GROUPS * (LAYERS + 1))
            sp.wait_ge(s_out, 16 * GROUPS)

        @blk.gpsimd
        def _(pool):
            G = nc.gpsimd
            G.memset(zeros[:, :], 0.0).then_inc(s_zero, 1)
            G.iota(iota_i[:, :], pattern=[[1, P]], base=0, channel_multiplier=0)
            G.iota(part_i[:, :], pattern=[[0, 1]], base=0, channel_multiplier=1)
            G.iota(base_i, pattern=[[ROWS, CHUNKS], [0, EPP]], base=0, channel_multiplier=0)
            G.iota(lost_i[:, :], pattern=[[P, EPP]], base=0, channel_multiplier=1)
            G.memset(ident[:, :], 0.0)
            G.memset(ones[:, :], 1.0).then_inc(s_const, 1)
            pool.wait_ge(s_const, 1)
            G.affine_select(out=ident[:, :], in_=ident[:, :], compare_op=ALU.not_equal, fill=1.0,
                            base=0, pattern=[[-1, P]], channel_multiplier=1)
            G.affine_select(out=before_f[:, :], in_=ones[:, :], compare_op=ALU.is_gt, fill=0.0,
                            base=0, pattern=[[1, P]], channel_multiplier=-1).then_inc(s_const, 1)
            last = slice((CHUNKS - 1) * EPP, EC)
            for n, (rows, fill) in enumerate(((dst_f, NOWHERE), (block_f, NO_BLOCK))):
                pool.wait_ge(s_masked, 2 * n + 1)
                G.affine_select(out=rows[:, last], in_=rows[:, last], compare_op=ALU.is_ge, fill=fill,
                                base=-OVERLAP, pattern=[[1, EPP]], channel_multiplier=EPP).then_inc(s_masked, 1)
            pool.wait_ge(s_cleared, 16)

            def scatter_records(k, s, use):
                pool.wait_ge(s_attr[s], use * 16)
                pool.wait_ge(s_row, k + 1)
                apart(pool)
                for t in range(EPP):
                    G.indirect_dma_start(out=records, out_offset=bass.IndirectOffsetOnAxis(ap=row_i[s][:, t:t + 1], axis=0),
                                         in_=rec[s][:, t, :], in_offset=None).then_inc(s_scat[s], 16)

            def gather_spare(s, use):
                pool.wait_ge(s_staged[s], use)
                apart(pool)
                for t in range(SPARE):
                    G.indirect_dma_start(out=gath[s][:, t * HID:(t + 1) * HID], out_offset=None, in_=table,
                                         in_offset=bass.IndirectOffsetOnAxis(ap=spare_now[s][:, t:t + 1], axis=0),
                                         ).then_inc(s_gath[s], 16)

            scatter_records(0, 0, 1)
            pool.wait_ge(s_table, 16 * GROUPS)
            with pool.Fori(0, PAIRS - 1) as i:
                scatter_records(i * 2 + 1, 1, i + 1)
                gather_spare(0, i + 1)
                scatter_records(i * 2 + 2, 0, i + 2)
                gather_spare(1, i + 1)
            scatter_records(CHUNKS - 1, 1, PAIRS)
            gather_spare(0, PAIRS)
            gather_spare(1, PAIRS)

            pool.wait_ge(s_flag, 1)
            flag = pool.value_load(flag_i[0:1, 0:1])
            with pool.Fori(0, LAYERS) as l:
                with pool.If(0 < flag):
                    with pool.Fori(0, EC) as n:
                        pool.wait_ge(s_gtile, l * EC + n + 1)
                        apart(pool)
                        G.indirect_dma_start(out=g_rows, out_offset=None, in_=table,
                                             in_offset=bass.IndirectOffsetOnAxis(ap=g_src[:, 0:1], axis=0)).then_inc(s_ggath, 16)
                n = (l + 1) * GROUPS
                for c in range(GROUPS + 2):
                    if c < GROUPS:
                        pool.wait_ge(s_h, n + c - GROUPS + 1)
                        G.tensor_tensor(out=tab_rows[:, c, :], in0=h_rows[:, c, :], in1=be_wide[:, :], op=ALU.add).then_inc(s_tab, 1)
                    if 1 <= c <= GROUPS:
                        cols = slice((c - 1) * GF, c * GF)
                        pool.wait_ge(s_parts, n + max(c - 2, 0))
                        pool.wait_ge(s_part1, n - GROUPS + c)
                        G.tensor_tensor(out=rest[c % 2][:, :], in0=tab_rows[:, c - 1, :], in1=parts[:, 0, cols], op=ALU.subtract).then_inc(s_rest, 1)
                    if c >= 2:
                        cols = slice((c - 2) * GF, (c - 1) * GF)
                        pool.wait_ge(s_part2, n - GROUPS + c - 1)
                        G.tensor_tensor(out=parts[:, 2, cols], in0=rest[(c - 1) % 2][:, :], in1=parts[:, 1, cols], op=ALU.subtract).then_inc(s_parts, 1)
                with pool.If(l < LAYERS - 1):
                    pool.wait_ge(s_table, (l + 2) * (16 * GROUPS))
                    apart(pool)
                    with pool.Fori(0, PAIRS) as i:
                        for s in range(2):
                            gather_spare(s, (l + 1) * PAIRS + i + 1)

        def start_sums(act, c, count):
            act.wait_ge(s_htr, count)
            nc.scalar.copy(z_cols[:, c * GN:(c + 1) * GN].rearrange("p (b n) -> p b n", b=BPG),
                           blocks(p_tr[:, 0:GF])[:, :, 0:NB]).then_inc(s_zc, 1)

        @blk.scalar
        def _(act):
            S = nc.scalar
            for c in range(GROUPS):
                start_sums(act, c, c + 1)

            def relu_batches(c, last_step):
                for b in range(ACT_BATCHES):
                    act.wait_ge(s_sc, c * BATCHES + b + 1)
                    act.wait_ge(s_sum, c * BATCHES + b + 1)
                    S.activation(msg[b % RING][:, :], bank(b % RING), ACT.Relu).then_inc(s_act, 1)
                    if b == 1:
                        last_step()

            def save_chunk(k, s):
                for b in range(4):
                    act.wait_ge(s_strp, k * 4 + b + 1)
                    lo, hi = b * 8, min(b * 8 + 8, TILES)
                    S.copy(stack_now[s][:, lo * P:hi * P], bank(2 + b % 2).bitcast(BF16)[0:STACK, 0:(hi - lo) * P]).then_inc(s_stc, 1)
                act.wait_ge(s_stc, (k + 1) * 4)
                act.dma_start(stacks[bass.ds(k, 1)].rearrange("o a b -> (o a) b"), stack_now[s][:, :]).then_inc(s_saved, 16)
                act.wait_ge(s_pick, (k + 1) * 7)
                act.dma_start(picks[bass.ds(k, 1)].rearrange("o a b -> (o a) b"), pick_now[s][:, :].bitcast(U8)).then_inc(s_saved, 16)

            with act.Fori(0, PAIRS) as i:
                for s in range(2):
                    k = i * 2 + s
                    save_chunk(k, s)
                    relu_batches(k, lambda: None)
                    act.wait_ge(s_saved, (k + 1) * 32)
                    act.sem_inc(s_savefree, 1)

            act.wait_ge(s_flag, 1)
            act.wait_ge(s_par, 16 * 6)

            def stage(k, s):
                S.copy(spare_now[s][:, :], spare_src[:, bass.ds(k * SPARE, SPARE)]).then_inc(s_staged[s], 1)

            stage(0, 0)
            with act.Fori(0, LAYERS) as l:
                S.copy(w_now[:, :], w12[:, bass.ds(l * (2 * HID), 2 * HID)]).then_inc(s_wnow, 1)
                n = l * GROUPS

                def hidden_relu(c):
                    act.wait_ge(s_hidp, n + c + 1)
                    if c:
                        act.wait_ge(s_z2p, n + c)
                    apart(act)
                    bias = b1_cols[:, bass.ds(l, 1)]
                    S.activation(hid[:, 0:GA], p_hid[:, 0:GA], ACT.Relu, bias=bias)
                    S.activation(hid[:, GA:GN], p_hid[:, 512:512 + GB], ACT.Relu, bias=bias).then_inc(s_hid, 1)

                hidden_relu(0)
                for c in range(GROUPS + 2):
                    if c + 1 < GROUPS:
                        hidden_relu(c + 1)
                    if c < GROUPS:
                        act.wait_ge(s_var, n + c + 1)
                        S.activation(std[:, :], mv[:, :, 1], ACT.Sqrt, bias=eps[:, 0:1]).then_inc(s_std, 1)
                    if 1 <= c <= GROUPS:
                        start_sums(act, c - 1, n + GROUPS + c)
                        cols = slice((c - 1) * GF, c * GF)
                        act.wait_ge(s_tab, n + GROUPS + c)
                        S.copy(parts[:, 0, cols], tab_rows[:, c - 1, :]).then_inc(s_part1, 1)
                    if c >= 2:
                        cols = slice((c - 2) * GF, (c - 1) * GF)
                        act.wait_ge(s_rest, n + c - 1)
                        S.copy(parts[:, 1, cols], rest[(c - 1) % 2][:, :]).then_inc(s_part2, 1)
                with act.If(l < LAYERS - 1):
                    with act.Fori(0, PAIRS) as i:
                        for s in range(2):
                            k = i * 2 + s
                            c = (l + 1) * CHUNKS + k

                            def next_rows():
                                act.wait_ge(s_left, c * 2 + 1)
                                apart(act)
                                stage(k + 1, 1 - s)

                            relu_batches(c, next_rows)
            for c in range(GROUPS):
                act.wait_ge(s_var, LAYERS * GROUPS + c + 1)
                S.activation(std[:, :], mv[:, :, 1], ACT.Sqrt, bias=eps[:, 0:1]).then_inc(s_std, 1)

        @blk.vector
        def _(dve):
            V = nc.vector
            TT = V.tensor_tensor
            prep = Chain(dve, s_prep)
            V.memset(eps[:, :], EPS)
            V.memset(z_cols[:, NODES:ZW], 0.0)
            for r in (*run, *orun):
                V.memset(r[:, 0:16] if len(r.shape) == 2 else r[:, 0:16, :], 0.0)
            V.memset(most[:, :], 0.0)
            dve.sem_inc(s_slotfree, 1)
            dve.sem_inc(s_savefree, 2)
            dve.sem_inc(s_left, 1)
            dve.sem_inc(s_added, 2)
            dve.sem_inc(s_gfree, 1)
            dve.sem_inc(s_gz, 1)
            dve.wait_ge(s_const, 2)
            V.tensor_copy(iota_f[:, :], iota_i[:, :])
            V.tensor_copy(part_f[:, :], part_i[:, :])
            V.tensor_copy(base_f[:, :], tmp_i[:, :])
            V.tensor_copy(ident_b[:, :], ident[:, :])
            V.tensor_copy(lost_f[:, :], lost_i[:, :])
            prep(V.tensor_copy(before[:, :], before_f[:, :]))
            for m in range(SPARE - 1):
                V.memset(steps_f[:, m:m + 1], float((m + 1) * P + 1))
            dve.wait_ge(s_ends, 64)
            prep(V.tensor_copy(dst_f[:, :], dst_i[:, :]))
            by_chunk = lambda a: a.rearrange("p (k t) -> p k t", t=EPP)
            V.tensor_reduce(ends[:, 0, :], by_chunk(dst_f[:, :]), axis=AX.X, op=ALU.min)
            prep(V.tensor_reduce(ends[:, 1, :], by_chunk(dst_f[:, :]), axis=AX.X, op=ALU.max))
            dve.wait_ge(s_prep_pe, 1)
            V.tensor_reduce(span[:, 0:1], bank(0)[0:CHUNKS, 0:P], axis=AX.X, op=ALU.min)
            prep(V.tensor_reduce(span[:, 1:2], bank(0)[0:CHUNKS, P:2 * P], axis=AX.X, op=ALU.max))
            prep(TT(out=span[:, 2:3], in0=span[:, 1:2], in1=span[:, 0:1], op=ALU.subtract))
            dve.wait_ge(s_prep_pe, 2)
            V.tensor_copy(first_i[:, :], bank(1)[0:1, 0:CHUNKS])
            prep(V.tensor_copy(first_row[:, :], bank(1)[0:1, 0:2 * CHUNKS]))
            dve.wait_ge(s_prep_pe, 3)
            prep(V.tensor_copy(first_all[:, :], bank(0)[:, 0:CHUNKS]))
            V.memset(meta[:, :, 3], 0.0)
            prep(V.scalar_tensor_tensor(out=meta[:, :, 1].rearrange("p (k t) -> p k t", t=EPP), in0=by_chunk(dst_f[:, :]), scalar=1.0,
                                        in1=first_all[:, :].unsqueeze(2).to_broadcast((P, CHUNKS, EPP)), op0=ALU.add, op1=ALU.subtract))
            dve.sem_inc(s_masked, 1)
            prep(V.tensor_copy(tmp_a[:, :], src_i[:, :]))
            prep(V.tensor_scalar(tmp_i[:, :], tmp_a[:, :], 1.0 / NB, 0.5 / NB - 0.5, ALU.mult, ALU.add))
            prep(V.tensor_copy(block_f[:, :], tmp_i[:, :]))
            prep(V.scalar_tensor_tensor(out=tmp_a[:, :], in0=block_f[:, :], scalar=-float(NB), in1=tmp_a[:, :], op0=ALU.mult, op1=ALU.add))
            prep(V.tensor_scalar(tmp_b[:, :], tmp_a[:, :], 0.0, None, ALU.is_lt))
            prep(V.scalar_tensor_tensor(out=tmp_b[:, :], in0=tmp_a[:, :], scalar=float(NB), in1=tmp_b[:, :], op0=ALU.is_ge, op1=ALU.subtract))
            TT(out=block_f[:, :], in0=block_f[:, :], in1=tmp_b[:, :], op=ALU.add)
            prep(V.scalar_tensor_tensor(out=tmp_a[:, :], in0=tmp_b[:, :], scalar=-float(NB), in1=tmp_a[:, :], op0=ALU.mult, op1=ALU.add))
            dve.wait_ge(s_masked, 2)
            V.tensor_copy(meta[:, :, 2].bitcast(I32), src_i[:, :])
            V.tensor_scalar(meta[:, :, 0], tmp_a[:, :], 1.0, None, ALU.add).then_inc(s_masked, 1)
            dve.wait_ge(s_masked, 4)

            RANK_STEPS = 29
            rank = Chain(dve, s_rank)

            def rank_chunk(k, s):
                rank.at(k * RANK_STEPS)
                edges = bass.ds(k * EPP, EPP)
                own_in = block_f[:, edges].unsqueeze(2).to_broadcast((P, EPP, BLOCKS))
                TT(out=own[:, :, :], in0=own_in, in1=iota_f[:, 0:BLOCKS].unsqueeze(1).to_broadcast((P, EPP, BLOCKS)), op=ALU.is_equal)
                rank(TT(out=run[0][:, 16:, :], in0=own_in, in1=iota_f[:, 0:BLOCKS].unsqueeze(1).to_broadcast((P, EPP, BLOCKS)), op=ALU.is_equal))
                for n, d in enumerate((1, 2, 4, 8, 16)):
                    a, b = run[n % 2], run[1 - n % 2]
                    rank(TT(out=b[:, 16:, :], in0=a[:, 16:, :], in1=a[:, 16 - d:16 - d + EPP, :], op=ALU.add))
                dve.sem_inc(s_tot, 1)
                dve.wait_ge(s_pre, 2 * k + 1)
                rank(TT(out=rank_w[:, :, :], in0=run[1][:, 16:, :], in1=bank(0)[:, 0:BLOCKS].unsqueeze(1).to_broadcast((P, EPP, BLOCKS)), op=ALU.add))
                rank(TT(out=rank_w[:, :, :], in0=rank_w[:, :, :], in1=own[:, :, :], op=ALU.mult))
                rank(V.tensor_reduce(rank1[:, :], rank_w[:, :, :], axis=AX.X, op=ALU.add))
                V.tensor_scalar(over[:, :], rank1[:, :], float(P + 1), None, ALU.is_ge)
                rank(V.tensor_scalar(orun[0][:, 16:], rank1[:, :], float(P + 1), None, ALU.is_ge))
                for n, d in enumerate((1, 2, 4, 8, 16)):
                    a, b = orun[n % 2], orun[1 - n % 2]
                    rank(TT(out=b[:, 16:], in0=a[:, 16:], in1=a[:, 16 - d:16 - d + EPP], op=ALU.add))
                rank(V.tensor_copy(otot[:, :], orun[1][:, 16 + EPP - 1:16 + EPP]))
                dve.sem_inc(s_tot, 1)
                dve.wait_ge(s_pre, 2 * k + 2)
                rank(V.scalar_tensor_tensor(out=rr[:, :], in0=orun[1][:, 16:], scalar=bank(1)[:, 0:1], in1=rank1[:, :], op0=ALU.add, op1=ALU.subtract))
                rank(TT(out=rr[:, :], in0=rr[:, :], in1=over[:, :], op=ALU.mult))
                rank(TT(out=rr[:, :], in0=rr[:, :], in1=rank1[:, :], op=ALU.add))
                TT(out=most[:, :], in0=most[:, :], in1=rr[:, :], op=ALU.max)
                rank(TT(out=steps_w[:, :, :], in0=rr[:, :].unsqueeze(2).to_broadcast((P, EPP, SPARE - 1)),
                        in1=steps_f[:, :].unsqueeze(1).to_broadcast((P, EPP, SPARE - 1)), op=ALU.is_ge))
                V.tensor_scalar(tile_f[:, :], block_f[:, edges], -1.0, float(BLOCKS), ALU.mult, ALU.add)
                rank(V.tensor_reduce(up[:, :], steps_w[:, :, :], axis=AX.X, op=ALU.add))
                TT(out=tile_f[:, :], in0=tile_f[:, :], in1=over[:, :], op=ALU.mult)
                rank(V.scalar_tensor_tensor(out=row_f[:, :], in0=up[:, :], scalar=-float(P), in1=rr[:, :], op0=ALU.mult, op1=ALU.add))
                TT(out=tile_f[:, :], in0=tile_f[:, :], in1=block_f[:, edges], op=ALU.add)
                rank(V.tensor_scalar(bad_f[:, :], rr[:, :], float(SPARE * P + 1), None, ALU.is_ge))
                TT(out=tile_f[:, :], in0=tile_f[:, :], in1=up[:, :], op=ALU.add)
                rank(V.scalar_tensor_tensor(out=bad_f[:, :], in0=rank1[:, :], scalar=1.0, in1=bad_f[:, :], op0=ALU.is_lt, op1=ALU.add))
                rank(V.scalar_tensor_tensor(out=row_f[:, :], in0=row_f[:, :], scalar=float(TILES), in1=tile_f[:, :], op0=ALU.mult, op1=ALU.add))
                V.tensor_scalar(up[:, :], row_f[:, :], -1.0, float(SLOTS + TILES), ALU.mult, ALU.add)
                rank(V.tensor_scalar(row_f[:, :], row_f[:, :], -float(TILES), None, ALU.add))
                rank(TT(out=up[:, :], in0=up[:, :], in1=lost_f[:, :], op=ALU.add))
                rank(TT(out=up[:, :], in0=up[:, :], in1=bad_f[:, :], op=ALU.mult))
                rank(TT(out=row_f[:, :], in0=row_f[:, :], in1=up[:, :], op=ALU.add))
                V.tensor_copy(rec[s][:, :, FEATS:REC].bitcast(I32), meta[:, edges, :].bitcast(I32))
                TT(out=row_i[s][:, :], in0=row_f[:, :], in1=base_f[:, edges], op=ALU.add).then_inc(s_row, 1)
                assert rank.n == RANK_STEPS, rank.n

            UNPACK_STEPS = 4
            unp = Chain(dve, s_unp)

            def unpack_chunk(k, s):
                unp.at(k * UNPACK_STEPS)
                stack = lambda n, m=1: stack_rows[:, :, n * FEATS:(n + m) * FEATS]
                feat = slots[:, :, 0:FEATS]
                dve.wait_ge(s_savefree, k + 1)
                dve.wait_ge(s_slot, (k + 1) * 16)
                apart(dve)
                V.tensor_copy(local_b[:, :], slots[:, 0:BLOCKS, FEATS]).then_inc(s_local, 1)
                unp(V.tensor_copy(stack(0), feat))
                unp(TT(out=a_left[:, :, :], in0=feat, in1=stack(0), op=ALU.subtract))
                V.tensor_copy(stack(1), stack(0))
                V.tensor_copy(stack(2), stack(0))
                unp(V.tensor_copy(stack(3), a_left[:, :, :]))
                V.tensor_copy(stack(4), stack(3))
                unp(TT(out=stack(5), in0=a_left[:, :, :], in1=stack(3), op=ALU.subtract))
                dve.sem_inc(s_stackrows, 1)
                V.tensor_copy(targets[:, bass.ds(k * TILES, TILES)], slots[:, :, FEATS + 1])
                V.tensor_copy(spare_now[s][:, :], slots[:, BLOCKS:TILES, FEATS + 2].bitcast(I32)).then_inc(s_staged[s], 1)
                V.tensor_copy(spare_src[:, bass.ds(k * SPARE, SPARE)], slots[:, BLOCKS:TILES, FEATS + 2].bitcast(I32)).then_inc(s_slotfree, 1)
                for b in range(7):
                    lo, hi = b * 4 * P, min(b * 4 + 4, BLOCKS) * P
                    dve.wait_ge(s_bc, k * 7 + b + 1)
                    apart(dve)
                    V.tensor_scalar(pick_now[s][:, lo:hi], bank(4 + b % 2)[0:NB, 0:hi - lo], part1[0:NB, 0:1], None, ALU.is_equal,
                                    saturate=False).then_inc(s_pick, 1)
                assert unp.n == UNPACK_STEPS

            V.tensor_scalar(iota1[:, :], iota_f[:, :], 1.0, None, ALU.add)
            prep(V.tensor_scalar(part1[:, :], part_f[:, :], 1.0, None, ALU.add))
            rank_chunk(0, 0)
            rank_chunk(1, 1)
            dve.wait_ge(s_we, 16 * (1 + STACK // FEATS))
            wr = we_rows
            prep(V.tensor_copy(we_stack[:, :], wr[:, 0, :]))
            prep(V.tensor_copy(wr[:, 1, :], we_stack[:, :]))
            prep(TT(out=wr[:, 3, :], in0=wr[:, 0, :], in1=wr[:, 1, :], op=ALU.subtract))
            prep(V.tensor_copy(we_stack[:, :], wr[:, 3, :]))
            prep(V.tensor_copy(wr[:, 2, :], we_stack[:, :]))
            prep(TT(out=wr[:, 3, :], in0=wr[:, 3, :], in1=wr[:, 2, :], op=ALU.subtract))
            for part in range(3):
                V.memset(part_sel[:, part:part + 1], 0.0)
            prep(V.tensor_scalar(part_sel[:, 3:4], part_f[0:STACK, :], 0.0, None, ALU.mult))
            for part, rows in enumerate(((0, 3, 5), (1, 4), (2,))):
                for r in rows:
                    prep(V.tensor_scalar(part_sel[:, 3:4], part_f[0:STACK, :], float(r * FEATS), None, ALU.is_ge))
                    prep(V.scalar_tensor_tensor(out=part_sel[:, 3:4], in0=part_f[0:STACK, :], scalar=float((r + 1) * FEATS),
                                                in1=part_sel[:, 3:4], op0=ALU.is_lt, op1=ALU.mult))
                    prep(TT(out=part_sel[:, part:part + 1], in0=part_sel[:, part:part + 1], in1=part_sel[:, 3:4], op=ALU.add))
            prep(V.tensor_scalar(wr[:, 0, :], wr[:, 1, :], part_sel[:, 0:1], None, ALU.mult))
            prep(V.scalar_tensor_tensor(out=wr[:, 0, :], in0=wr[:, 2, :], scalar=part_sel[:, 1:2], in1=wr[:, 0, :], op0=ALU.mult, op1=ALU.add))
            prep(V.scalar_tensor_tensor(out=we_stack[:, :], in0=wr[:, 3, :], scalar=part_sel[:, 2:3], in1=wr[:, 0, :], op0=ALU.mult, op1=ALU.add))

            dve.wait_ge(s_x, 16 * (GROUPS + 1))
            prep(V.tensor_copy(be_wide[:, :].rearrange("p (b f) -> p b f", b=BPG), be_all[:, :].unsqueeze(1).to_broadcast((NB, BPG, HID))))
            for c in range(GROUPS):
                cols = slice(c * GF, (c + 1) * GF)
                V.tensor_copy(h_rows[:, c, :], x_rows[:, c, :])
                TT(out=tab_rows[:, c, :], in0=x_rows[:, c, :], in1=be_wide[:, :], op=ALU.add).then_inc(s_tab, 1)
                dve.wait_ge(s_tab, c + 1)
                prep(V.tensor_copy(parts[:, 0, cols], tab_rows[:, c, :]))
                prep(TT(out=zn[:, :], in0=tab_rows[:, c, :], in1=parts[:, 0, cols], op=ALU.subtract))
                prep(V.tensor_copy(parts[:, 1, cols], zn[:, :]))
                TT(out=parts[:, 2, cols], in0=zn[:, :], in1=parts[:, 1, cols], op=ALU.subtract).then_inc(s_parts, 1)
                dve.wait_ge(s_parts, c + 1)

            def edge_chunk(k, s, c, use):
                node = dve.value_load(first_i[0:1, bass.ds(k, 1)], min_val=0, max_val=NODES - 1)
                for b in range(BATCHES):
                    n = min(TB, TILES - b * TB)
                    dve.wait_ge(s_sc, c * BATCHES + b + 1)
                    TT(out=hot[b % RING][:, 0:n, :], in0=iota1[:, :].unsqueeze(1).to_broadcast((P, n, WIN)),
                       in1=targets[:, bass.ds(k * TILES + b * TB, n)].unsqueeze(2).to_broadcast((P, n, WIN)),
                       op=ALU.is_equal).then_inc(s_hot, 1)
                    if b < ACT_BATCHES:
                        continue
                    own_cols = HID * (BLOCKS - b * TB) if b == ACT_BATCHES else 0
                    at = HID * (b * TB - BLOCKS) + own_cols
                    dve.wait_ge(s_gath[s], use * (16 * SPARE))
                    dve.wait_ge(s_sum, c * BATCHES + b + 1)
                    m = msg[b % RING]
                    if own_cols:
                        V.tensor_scalar(m[:, 0:own_cols], bank(b % RING)[:, 0:own_cols], 0.0, None, ALU.max)
                    TT(out=m[:, own_cols:n * HID], in0=bank(b % RING)[:, own_cols:n * HID],
                       in1=gath[s][:, at:at + n * HID - own_cols], op=ALU.add).then_inc(s_leftstep, 1)
                    dve.wait_ge(s_leftstep, c * 2 + (b - ACT_BATCHES + 1))
                    V.tensor_scalar(m[:, own_cols:n * HID], m[:, own_cols:n * HID], 0.0, None, ALU.max).then_inc(s_left, 1)
                dve.wait_ge(s_sc, (c + 1) * BATCHES + RING)
                TT(out=z_cols[:, bass.ds(node, WIN)], in0=z_cols[:, bass.ds(node, WIN)], in1=p_win[s][:, 0:WIN],
                   op=ALU.add).then_inc(s_added, 1)
                dve.wait_ge(s_added, c + 3)
                apart(dve)

            dve.wait_ge(s_zc, GROUPS)
            with dve.Fori(0, PAIRS - 1) as i:
                for s in range(2):
                    k = i * 2 + s
                    unpack_chunk(k, s)
                    rank_chunk(k + 2, s)
                    edge_chunk(k, s, k, i + 1)
            for s in range(2):
                k = CHUNKS - 2 + s
                unpack_chunk(k, s)
                edge_chunk(k, s, k, PAIRS)

            n_prep = prep.n
            V.tensor_reduce(most1[:, :], most[:, :], axis=AX.X, op=ALU.max).then_inc(s_tot, 1)
            dve.wait_ge(s_slotfree, CHUNKS + 1)
            V.tensor_copy(spare_src[:, CHUNKS * SPARE:], spare_src[:, 0:SPARE])
            dve.wait_ge(s_prep_pe, 4)
            V.tensor_reduce(flag_f[:, 0:1], first_row[0:1, CHUNKS:2 * CHUNKS], axis=AX.X, op=ALU.max)
            prep(V.tensor_reduce(flag_f[:, 1:2], bank(0)[0:1, 0:P], axis=AX.X, op=ALU.max))
            prep(V.tensor_scalar(flag_f[:, 0:1], flag_f[:, 0:1], float(WIN), None, ALU.is_ge))
            prep(V.tensor_scalar(flag_f[:, 1:2], flag_f[:, 1:2], float(SPARE * P + 1), None, ALU.is_ge))
            TT(out=flag_i[:, :], in0=flag_f[:, 0:1], in1=flag_f[:, 1:2], op=ALU.add).then_inc(s_flag, 1)

            dve.wait_ge(s_flag, 1)
            flag = dve.value_load(flag_i[0:1, 0:1])
            upd = Chain(dve, s_upd)
            UPD_STEPS = 4

            def statistics(z, count):
                for b in range(BPG):
                    last = V.bn_stats(stats[:, b, :], z[:, b * HID:(b + 1) * HID])
                upd(last)
                apart(dve)
                for b in range(BPG):
                    last = V.bn_aggr(mv[:, b, :], stats[:, b, :])
                last.then_inc(s_var, 1)
                dve.wait_ge(s_std, count)
                upd(V.reciprocal(rstd[:, :], std[:, :]))

            with dve.Fori(0, LAYERS) as l:
                with dve.If(0 < flag):
                    for c in range(GROUPS):
                        dve.wait_ge(s_gtrh, l * GROUPS + c + 1)
                        V.tensor_copy(z_cols[:, c * GN:(c + 1) * GN].rearrange("p (b n) -> p b n", b=BPG),
                                      blocks(p_tr[:, 0:GF])[:, :, 0:NB]).then_inc(s_gz, 1)
                    gen = Chain(dve, s_gstep)

                    with dve.Fori(0, CHUNKS) as k:
                        dve.wait_ge(s_gattr, (l * CHUNKS + k + 1) * 16)
                        apart(dve)
                        with dve.Fori(0, EPP) as t:
                            n = l * EC + k * EPP + t
                            gen.at(n)
                            at = k * EPP + t
                            V.tensor_copy(g_feat[:, :], g_attr[:, bass.ds(t * FEATS, FEATS)])
                            V.tensor_copy(g_dst[:, :], dst_f[:, bass.ds(at, 1)])
                            V.tensor_copy(g_src[:, :], src_i[:, bass.ds(at, 1)]).then_inc(s_gtile, 1)
                            dve.wait_ge(s_gtr, n + 1)
                            V.tensor_copy(g_cols[:, :], bank(0)[0:FEATS, 0:P]).then_inc(s_gcols, 1)
                            dve.wait_ge(s_ggath, (n + 1) * 16)
                            dve.wait_ge(s_gterm, n + 1)
                            gen(TT(out=g_msg, in0=g_rows, in1=bank(1)[:, 0:HID], op=ALU.add))
                            V.tensor_scalar(g_msg, g_msg, 0.0, None, ALU.max).then_inc(s_gmsg, 1)
                            with dve.Fori(0, WINDOWS) as w:
                                m = n * WINDOWS + w
                                V.tensor_scalar(g_hot, iota_f[:, :], g_dst[:, 0:1], None, ALU.is_equal).then_inc(s_ghot, 1)
                                dve.wait_ge(s_gwin, m + 1)
                                V.tensor_scalar(g_dst[:, :], g_dst[:, :], -float(WIN), None, ALU.add)
                                TT(out=z_cols[:, bass.ds(w * WIN, WIN)], in0=z_cols[:, bass.ds(w * WIN, WIN)], in1=p_win[0][:, 0:WIN],
                                   op=ALU.add).then_inc(s_gadd, 1)
                                dve.wait_ge(s_gadd, m + 1)
                                apart(dve)
                        dve.sem_inc(s_gfree, 1)

                for c in range(GROUPS):
                    n = l * GROUPS + c
                    z = p_z2[c % 2][0:NB, 0:GF]
                    upd.at(n * UPD_STEPS)
                    dve.wait_ge(s_z2p, n + 1)
                    statistics(z, n + 1)
                    for b in range(BPG):
                        row = slice(b * HID, (b + 1) * HID)
                        last = V.scalar_tensor_tensor(out=zn[:, row], in0=z[:, row], scalar=mv[:, b, 0:1],
                                                      in1=g_all[:, bass.ds(l * HID, HID)], op0=ALU.subtract, op1=ALU.mult)
                    upd(last)
                    dve.sem_inc(s_z2, 1)
                    for b in range(BPG):
                        row = slice(b * HID, (b + 1) * HID)
                        last = V.scalar_tensor_tensor(out=zn[:, row], in0=zn[:, row], scalar=rstd[:, b:b + 1],
                                                      in1=b_all[:, bass.ds(l * HID, HID)], op0=ALU.mult, op1=ALU.add)
                    upd(last)
                    V.scalar_tensor_tensor(out=h_rows[:, c, :], in0=zn[:, :], scalar=0.0, in1=h_rows[:, c, :],
                                           op0=ALU.max, op1=ALU.add).then_inc(s_h, 1)
                    assert upd.n == UPD_STEPS
                with dve.If(l < LAYERS - 1):
                    dve.wait_ge(s_zc, (l + 2) * GROUPS)
                    apart(dve)
                    with dve.Fori(0, PAIRS) as i:
                        for s in range(2):
                            k = i * 2 + s
                            edge_chunk(k, s, (l + 1) * CHUNKS + k, (l + 1) * PAIRS + i + 1)
            upd.at(LAYERS * GROUPS * UPD_STEPS)
            for c in range(GROUPS):
                if c:
                    dve.wait_ge(s_final, c)
                upd(TT(out=z2[:, :], in0=x_rows[:, c, :], in1=h_rows[:, c, :], op=ALU.add))
                statistics(z2, LAYERS * GROUPS + c + 1)
                for b in range(BPG):
                    row = slice(b * HID, (b + 1) * HID)
                    last = V.tensor_scalar(x_rows[:, c, row], z2[:, row], mv[:, b, 0:1], rstd[:, b:b + 1], ALU.subtract, ALU.mult)
                last.then_inc(s_final, 1)

        @blk.tensor
        def _(pe):
            T = nc.tensor

            def transpose_h(rows):
                for b in range(BPG):
                    last = T.transpose(p_tr[:, b * HID:b * HID + NB], rows[:, b * HID:(b + 1) * HID], ident[0:NB, 0:NB])
                last.then_inc(s_htr, 1)

            pe.wait_ge(s_const, 2)
            pe.wait_ge(s_prep, 3)
            T.transpose(bank(0)[0:CHUNKS, 0:P], ends[:, 0, :], ident[:, :])
            T.transpose(bank(0)[0:CHUNKS, P:2 * P], ends[:, 1, :], ident[:, :]).then_inc(s_prep_pe, 1)
            pe.wait_ge(s_prep, 5)
            T.transpose(bank(1)[0:1, 0:CHUNKS], span[:, 0:1], ident[0:CHUNKS, 0:CHUNKS])
            T.transpose(bank(1)[0:1, CHUNKS:2 * CHUNKS], span[:, 2:3], ident[0:CHUNKS, 0:CHUNKS]).then_inc(s_prep_pe, 1)
            pe.wait_ge(s_prep, 6)
            T.matmul(bank(0)[:, 0:CHUNKS], ones[0:1, :], first_row[0:1, 0:CHUNKS], start=True, stop=True).then_inc(s_prep_pe, 1)
            pe.wait_ge(s_x, 16 * (GROUPS + 1))
            for c in range(GROUPS):
                if c:
                    pe.wait_ge(s_zc, c)
                transpose_h(x_rows[:, c, :])
            pe.wait_ge(s_prep, 7)

            def rank_products(k):
                pe.wait_ge(s_tot, 2 * k + 1)
                T.matmul(bank(0)[:, 0:BLOCKS], before[:, :], run[1][:, 16 + EPP - 1, :], start=True, stop=True).then_inc(s_pre, 1)
                pe.wait_ge(s_tot, 2 * k + 2)
                T.matmul(bank(1)[:, 0:1], before[:, :], otot[:, :], start=True, stop=True).then_inc(s_pre, 1)

            def unpack_products(k):
                pe.wait_ge(s_local, k + 1)
                for b in range(7):
                    if b >= 2:
                        pe.wait_ge(s_pick, k * 7 + b - 1)
                    for j in range(b * 4, min(b * 4 + 4, BLOCKS)):
                        last = T.matmul(bank(4 + b % 2)[:, (j % 4) * P:(j % 4 + 1) * P], local_b[:, j:j + 1].to_broadcast((P, P)),
                                        ident_b[:, :], start=True, stop=True)
                    last.then_inc(s_bc, 1)
                pe.wait_ge(s_stackrows, k + 1)
                for b in range(4):
                    if b >= 2:
                        pe.wait_ge(s_stc, k * 4 + b - 1)
                    for j in range(b * 8, min(b * 8 + 8, TILES)):
                        last = T.transpose(bank(2 + b % 2).bitcast(BF16)[0:STACK, (j % 8) * P:(j % 8 + 1) * P],
                                           stack_rows[:, j, :], ident_b[:, :])
                    last.then_inc(s_strp, 1)

            pe.sem_inc(s_sc, RING)

            def edge_chunk(s, c, parts_base):
                def sums(b):
                    if parts_base is not None and b < ACT_BATCHES:
                        pe.wait_ge(s_parts, parts_base + min((b + 1) * TB - 1, BLOCKS - 1) // BPG + 1)
                        apart(pe)
                    for j in range(b * TB, min((b + 1) * TB, TILES)):
                        to = bank(b % RING)[:, (j - b * TB) * HID:(j - b * TB + 1) * HID]
                        if j < BLOCKS:
                            for part in range(3):
                                T.matmul(to, pick_now[s][:, j * P:(j + 1) * P], parts[:, part, j * HID:(j + 1) * HID],
                                         start=(part == 0), stop=False)
                        last = T.matmul(to, stack_now[s][:, j * P:(j + 1) * P], we_stack[:, :], start=(j >= BLOCKS), stop=True)
                    last.then_inc(s_sum, 1)

                def scatter(b):
                    pe.wait_ge(s_hot, c * BATCHES + b + 1)
                    if b < ACT_BATCHES:
                        pe.wait_ge(s_act, c * ACT_BATCHES + b + 1)
                    else:
                        pe.wait_ge(s_left, c * 2 + (b - ACT_BATCHES) + 2)
                    for j in range(b * TB, min((b + 1) * TB, TILES)):
                        m = j - b * TB
                        last = T.matmul(p_win[s][:, 0:WIN], msg[b % RING][:, m * HID:(m + 1) * HID], hot[b % RING][:, m, :],
                                        start=(j == 0), stop=(j == TILES - 1))
                    last.then_inc(s_sc, 1)

                sums(0)
                for b in range(1, BATCHES):
                    sums(b)
                    if b == 1:
                        pe.wait_ge(s_added, c + 1)
                    scatter(b - 1)
                scatter(BATCHES - 1)

            rank_products(0)
            rank_products(1)
            pe.wait_ge(s_parts, GROUPS)
            with pe.Fori(0, PAIRS - 1) as i:
                for s in range(2):
                    k = i * 2 + s
                    unpack_products(k)
                    rank_products(k + 2)
                    pe.wait_ge(s_row, k + 3)
                    pe.wait_ge(s_stc, (k + 1) * 4)
                    pe.wait_ge(s_pick, (k + 1) * 7)
                    apart(pe)
                    edge_chunk(s, k, None)
            for s in range(2):
                k = CHUNKS - 2 + s
                unpack_products(k)
                pe.wait_ge(s_stc, (k + 1) * 4)
                pe.wait_ge(s_pick, (k + 1) * 7)
                edge_chunk(s, k, None)
            pe.wait_ge(s_tot, 2 * CHUNKS + 1)
            T.transpose(bank(0)[0:1, 0:P], most1[:, :], ident[:, :]).then_inc(s_prep_pe, 1)

            pe.wait_ge(s_flag, 1)
            flag = pe.value_load(flag_i[0:1, 0:1])

            with pe.Fori(0, LAYERS) as l:
                with pe.If(0 < flag):
                    for c in range(GROUPS):
                        pe.wait_ge(s_gz, l * GROUPS + c + 1)
                        for b in range(BPG):
                            last = T.transpose(p_tr[:, b * HID:b * HID + NB], h_rows[:, c, b * HID:(b + 1) * HID], ident[0:NB, 0:NB])
                        last.then_inc(s_gtrh, 1)
                    with pe.Fori(0, EC) as t:
                        n = l * EC + t
                        pe.wait_ge(s_gtile, n + 1)
                        T.transpose(bank(0)[0:FEATS, 0:P], g_feat[:, :], ident[:, :]).then_inc(s_gtr, 1)
                        pe.wait_ge(s_gcols, n + 1)
                        T.matmul(bank(1)[:, 0:HID], g_cols[:, :], we_f[:, :], start=True, stop=True).then_inc(s_gterm, 1)
                        pe.wait_ge(s_gmsg, n + 1)
                        apart(pe)
                        with pe.Fori(0, WINDOWS) as w:
                            pe.wait_ge(s_ghot, n * WINDOWS + w + 1)
                            T.matmul(p_win[0][:, 0:WIN], g_msg, g_hot, start=True, stop=True).then_inc(s_gwin, 1)
                    pe.wait_ge(s_gadd, (l + 1) * (EC * WINDOWS))
                    apart(pe)

                def hidden(c):
                    T.matmul(p_hid[:, 0:GA], w_now[:, 0:HID], z_cols[:, c * GN:c * GN + GA], start=True, stop=True)
                    T.matmul(p_hid[:, 512:512 + GB], w_now[:, 0:HID], z_cols[:, c * GN + GA:(c + 1) * GN],
                             start=True, stop=True).then_inc(s_hidp, 1)

                pe.wait_ge(s_added, (l + 1) * CHUNKS + 2)
                pe.wait_ge(s_wnow, l + 1)
                n = l * GROUPS
                hidden(0)
                for c in range(GROUPS):
                    pe.wait_ge(s_hid, n + c + 1)
                    if c >= 2:
                        pe.wait_ge(s_z2, n + c - 1)
                    z = p_z2[c % 2][0:NB, :]
                    for b in range(BPG):
                        T.matmul(z[:, b * HID:(b + 1) * HID], hid[:, b * NB:(b + 1) * NB], w_now[:, HID:2 * HID], start=True, stop=False)
                        last = T.matmul(z[:, b * HID:(b + 1) * HID], ones[0:1, 0:NB], b2_row[0:1, bass.ds(l * HID, HID)],
                                        start=False, stop=True)
                    last.then_inc(s_z2p, 1)
                    if c + 1 < GROUPS:
                        hidden(c + 1)
                    if c:
                        pe.wait_ge(s_h, n + c)
                        pe.wait_ge(s_zc, n + GROUPS + c - 1)
                        transpose_h(h_rows[:, c - 1, :])
                pe.wait_ge(s_h, n + GROUPS)
                pe.wait_ge(s_zc, n + 2 * GROUPS - 1)
                transpose_h(h_rows[:, GROUPS - 1, :])
                with pe.If(l < LAYERS - 1):
                    with pe.Fori(0, PAIRS) as i:
                        for s in range(2):
                            c = (l + 1) * CHUNKS + i * 2 + s
                            pe.wait_ge(s_str[s], (l * PAIRS + i + 1) * 32)
                            apart(pe)
                            edge_chunk(s, c, (l + 1) * GROUPS)


_INS = ["x", "src", "dst", "edge_attr_16", "L0_gnn_We", "L0_gnn_be", "L0_gnn_W1", "L0_gnn_b1", "L0_gnn_W2", "L0_gnn_b2",
        "L0_gnn_ln_g", "L0_gnn_ln_b"]


def kernel(**inputs):
    import numpy as _np
    import concourse.bacc as _bacc
    from concourse import mybir as _mybir
    from concourse.bass_utils import run_bass_kernel_spmd as _run

    nc = _bacc.Bacc("TRN2", target_bir_lowering=False, num_devices=1)
    arrays, args = {}, []
    for name in _INS:
        a = _np.ascontiguousarray(inputs[name])
        arrays[f"in_{name}"] = a
        args.append(nc.dram_tensor(f"in_{name}", a.shape, _mybir.dt.from_np(a.dtype), kind="ExternalInput").ap())
    args.append(nc.dram_tensor("out", (NODES, HID), F32, kind="ExternalOutput").ap())
    gnn_kernel(nc, *args)
    r = _run(nc, [arrays], core_ids=[0])
    return r.results[0]["out"]
```

```python
import concourse.bass as bass
from concourse import mybir
from contextlib import ExitStack

F32 = mybir.dt.float32
BF16 = mybir.dt.bfloat16
FP8 = mybir.dt.float8e4
U8 = mybir.dt.uint8
I32 = mybir.dt.int32
ALU = mybir.AluOpType
ACT = mybir.ActivationFunctionType
AX = mybir.AxisListType

NODES, HID = 3125, 128
EDGES, FEATS = 103125, 16
LAYERS = 4
EPS = 1e-5
P = 128

NB = 125
BLOCKS = NODES // NB
BPG = 5
GROUPS = BLOCKS // BPG
GN = NB * BPG
GF = BPG * HID
GA, GB = 3 * NB, 2 * NB

EPP = 29
CE = P * EPP
CHUNKS = -(-EDGES // CE)
TAIL0 = EDGES - CE
OVERLAP = (CHUNKS - 1) * CE - TAIL0
DIRECT = 6
SORTED = EPP - DIRECT
SPARE = 1
FILLED = BLOCKS + SPARE
FETCHED = SPARE + DIRECT
TILES = FILLED + DIRECT
SLOTS = P * TILES
SORT_SLOTS = P * FILLED
ROWS = SORT_SLOTS + P * SORTED
REC = 20
TB = 4
BATCHES = -(-TILES // TB)
ACT_BATCHES = BLOCKS // TB
RING = 4
FIRST_PART = 17
AHEAD = 2
WIN = 128
ZW = NODES + WIN
WINDOWS = -(-NODES // WIN)
PAIRS = CHUNKS // 2
STACK = 6 * FEATS
NO_BLOCK, NOWHERE = 31.0, -1.0e6
assert CHUNKS == 2 * PAIRS and GROUPS * BPG == BLOCKS and BLOCKS == ACT_BATCHES * TB + 1
assert SPARE == 1 and BATCHES == ACT_BATCHES + 2 == 8 and BATCHES % RING == 0


class Chain:

    def __init__(self, eng, sem):
        self.eng, self.sem, self.base, self.n = eng, sem, 0, 0

    def at(self, base):
        self.base, self.n = base, 0

    def __call__(self, ins):
        self.n += 1
        ins.then_inc(self.sem, 1)
        self.eng.wait_ge(self.sem, self.base + self.n)


def gnn_kernel(nc, x, src, dst, attr, we, be, w1, b1, w2, b2, ln_g, ln_b, out):
    ctx = ExitStack()
    with ctx:
        def sb(name, shape, dt=F32):
            return ctx.enter_context(nc.sbuf_tensor(name, shape, dt))

        def sem(name):
            return ctx.enter_context(nc.semaphore(name))

        table = nc.dram_tensor("table", (NODES, HID), F32, kind="Internal").ap()
        records = nc.dram_tensor("records", (CHUNKS * ROWS, REC), F32, kind="Internal").ap()
        stacks = nc.dram_tensor("stacks", (CHUNKS, STACK, SLOTS), BF16, kind="Internal").ap()
        picks = nc.dram_tensor("picks", (CHUNKS, NB, BLOCKS * P), U8, kind="Internal").ap()

        ident = sb("ident", [P, P])
        ident_b = sb("ident_b", [P, P], BF16)
        ones = sb("ones", [P, P])
        before = sb("before", [P, P], BF16)
        before_f = sb("before_f", [P, P])
        iota_i = sb("iota_i", [P, P], I32)
        iota_f = sb("iota_f", [P, P])
        part_i = sb("part_i", [P, 1], I32)
        part_f = sb("part_f", [P, 1])
        part1 = sb("part1", [P, 1])
        iota1 = sb("iota1", [P, WIN])
        lost_i = sb("lost_i", [P, SORTED], I32)
        lost_f = sb("lost_f", [P, SORTED])
        base_f = sb("base_f", [P, CHUNKS * EPP])
        we_f = sb("we_f", [FEATS, HID])
        we_rows = sb("we_rows", [STACK, 4, HID])
        we_stack = sb("we_stack", [STACK, HID], BF16)
        part_sel = sb("part_sel", [STACK, 4])
        w12 = sb("w12", [P, LAYERS * 2 * HID])
        w_now = sb("w_now", [P, 2 * HID])
        b1_cols = sb("b1_cols", [P, LAYERS])
        b2_rows = sb("b2_rows", [3, LAYERS * HID])
        b2_parts = sb("b2_parts", [3, LAYERS * HID], BF16)
        ones_b = sb("ones_b", [3, NB], BF16)
        part_is = sb("part_is", [3, 3])
        g_all = sb("g_all", [NB, LAYERS * HID])
        b_all = sb("b_all", [NB, LAYERS * HID])
        be_all = sb("be_all", [NB, HID])
        be_wide = sb("be_wide", [NB, GF])
        eps = sb("eps", [NB, 1])
        root_ready = sb("root_ready", [NB, 1])
        zeros = sb("zeros", [P, FILLED * REC])

        EC = CHUNKS * EPP
        src_i = sb("src_i", [P, EC], I32)
        dst_i = sb("dst_i", [P, EC], I32)
        block_all = sb("block_f", [P, EC + SORTED])
        block_f = block_all[:, 0:EC]
        dst_f = sb("dst_f", [P, EC])
        tmp_a = sb("tmp_a", [P, EC])
        tmp_b = sb("tmp_b", [P, EC])
        tmp_i = sb("tmp_i", [P, EC], I32)
        base_i = tmp_i[:, :].rearrange("p (k t) -> p k t", t=EPP)
        meta = sb("meta", [P, EC, 4])
        ends = sb("ends", [P, 2, CHUNKS])
        span = sb("span", [CHUNKS, 4])
        first_row = sb("first_row", [1, 2 * CHUNKS])
        first_i = sb("first_i", [1, CHUNKS], I32)
        first_all = sb("first_all", [P, CHUNKS])
        own = sb("own", [P, BLOCKS, SORTED], BF16)
        run = sb("run", [P, BLOCKS, SORTED], BF16)
        goes_on = sb("goes_on", [P, BLOCKS, SORTED], BF16)
        rank_w = sb("rank_w", [P, BLOCKS, SORTED])
        rank1 = sb("rank1", [P, SORTED])
        over = sb("over", [P, SORTED])
        over_run = sb("over_run", [P, SORTED], BF16)
        rr = sb("rr", [P, SORTED])
        up = sb("up", [P, SORTED])
        tile_f = sb("tile_f", [P, SORTED])
        row_f = sb("row_f", [P, SORTED])
        bad_f = sb("bad_f", [P, SORTED])
        most = sb("most", [P, SORTED])
        most1 = sb("most1", [P, 1])
        flag_f = sb("flag_f", [1, 2])
        flag_i = sb("flag_i", [1, 1], I32)
        row_i = [sb(f"row_i{n}", [P, SORTED], I32) for n in range(2)]
        rec = [sb(f"rec{n}", [P, EPP, REC]) for n in range(2)]
        slots = sb("slots", [P, TILES, REC])
        stack_rows = sb("stack_rows", [P, TILES, STACK], BF16)
        a_left = sb("a_left", [P, TILES, FEATS])
        local_b = sb("local_b", [P, BLOCKS], BF16)
        targets = sb("targets", [P, CHUNKS * TILES + TB])
        spare_src = sb("spare_src", [P, (CHUNKS + 1) * FETCHED], I32)

        stack_now = [sb(f"stack_now{n}", [STACK, SLOTS], BF16) for n in range(2)]
        pick_now = [sb(f"pick_now{n}", [NB, BLOCKS * P], FP8) for n in range(2)]
        spare_now = [sb(f"spare_now{n}", [P, FETCHED], I32) for n in range(2)]
        gath = [sb(f"gath{n}", [P, FETCHED * HID]) for n in range(2)]
        msg = [sb(f"msg{n}", [P, TB * HID]) for n in range(RING)]
        hot = [sb(f"hot{n}", [P, TB, WIN]) for n in range(RING)]

        x_rows = sb("x_rows", [NB, GROUPS, GF])
        h_rows = sb("h_rows", [NB, GROUPS, GF])
        tab_rows = sb("tab_rows", [NB, GROUPS, GF])
        parts = sb("parts", [NB, 3, GROUPS * GF], BF16)
        z_cols = sb("z_cols", [P, ZW])
        after_ranks = meta[:, :, :].rearrange("p e w -> p (e w)")
        rest = [after_ranks[0:NB, n * GF:(n + 1) * GF] for n in range(2)]
        hid = after_ranks[:, 2 * GF:2 * GF + GN]
        zn = [tmp_a[0:NB, 0:GF], tmp_b[0:NB, 0:GF]]
        stats = sb("stats", [NB, BPG, 6])
        mv = [sb(f"mv{n}", [NB, BPG, 2]) for n in range(2)]
        std = [sb(f"std{n}", [NB, BPG]) for n in range(2)]
        rstd = [sb(f"rstd{n}", [NB, BPG]) for n in range(2)]
        shift = [sb(f"shift{n}", [NB, BPG]) for n in range(2)]

        g_attr = rec[0][:, :, :].rearrange("p t w -> p (t w)")[:, 0:EPP * FEATS]
        g_src = sb("g_src", [P, 1], I32)
        g_dst = sb("g_dst", [P, 1])
        g_feat = sb("g_feat", [P, FEATS])
        g_cols = sb("g_cols", [FEATS, P])
        g_rows = gath[0][:, 0:HID]
        g_msg = msg[0][:, 0:HID]
        g_hot = hot[0][:, 0, :]

        psum = ctx.enter_context(nc.psum_tensor("psum", [P, 8 * 512], F32))
        bank = lambda n, m=1: psum[:, n * 512:(n + m) * 512]
        p_hid, p_z2, p_tr = bank(0, 2), [bank(2, 2), bank(4, 2)], bank(6, 2)
        p_win = [bank(4), bank(5)]
        p_before = [bank(6), bank(7)]

        s_const = sem("consts_made")
        s_zero = sem("zeros_made")
        s_ends = sem("ends_loaded")
        s_x = sem("x_loaded")
        s_we = sem("we_loaded")
        s_par = sem("params_loaded")
        s_cleared = [sem(f"records_cleared{n}") for n in range(2)]
        s_prep = sem("prep_steps")
        s_prep_pe = sem("prep_products")
        s_masked = sem("overlap_masked")
        s_attr = [sem(f"attr_loaded{n}") for n in range(2)]
        s_rank = sem("rank_steps")
        s_tot = sem("totals_ready")
        s_pre = sem("totals_before")
        s_row = sem("rows_ready")
        s_scat = [sem(f"records_scattered{n}") for n in range(2)]
        s_slot = sem("slots_loaded")
        s_slotfree = sem("slots_used")
        s_unp = sem("unpack_steps")
        s_stackrows = sem("stack_rows_ready")
        s_local = sem("locals_ready")
        s_bc = sem("locals_spread")
        s_pick = sem("picks_ready")
        s_strp = sem("stack_transposed")
        s_stc = sem("stack_copied")
        s_saved = sem("chunk_saved")
        s_savefree = sem("save_place_free")
        s_flag = sem("flag_ready")

        s_str = [sem(f"stream_loaded{n}") for n in range(2)]
        s_staged = [sem(f"spare_staged{n}") for n in range(2)]
        s_gath = [sem(f"rows_gathered{n}") for n in range(2)]
        s_sum = sem("sums_ready")
        s_act = sem("messages_ready")
        s_left = sem("spare_messages_ready")
        s_leftstep = sem("spare_sums_ready")
        s_hot = sem("one_hot_ready")
        s_sc = sem("batch_scattered")
        s_added = sem("window_added")
        s_again = sem("first_targets_again")

        s_wnow = sem("weights_staged")
        s_hidp = sem("hidden_summed")
        s_hid = sem("hidden_ready")
        s_z2p = sem("update_summed")
        s_upd = sem("update_steps")
        s_var = sem("variance_ready")
        s_std = sem("deviation_ready")
        s_scale = sem("scale_ready")
        s_norm = sem("normalized")
        s_h0 = sem("h_started")
        s_h = sem("h_ready")
        s_tab = sem("table_rows_ready")
        s_parts = sem("parts_ready")
        s_part1 = sem("part_1_ready")
        s_part2 = sem("part_2_ready")
        s_rest = sem("rest_ready")
        s_htr = sem("h_transposed")
        s_zc = sem("sums_started")
        s_table = sem("table_written")
        s_out = sem("output_written")
        s_apart = sem("waits_done")

        s_gtrh = sem("general_h_transposed")
        s_gz = sem("general_sums_started")
        s_gattr = sem("general_attr")
        s_gfree = sem("general_attr_used")
        s_gtile = sem("general_tile")
        s_gtr = sem("general_transposed")
        s_gcols = sem("general_cols")
        s_gterm = sem("general_term")
        s_ggath = sem("general_gathered")
        s_gmsg = sem("general_message")
        s_ghot = sem("general_one_hot")
        s_gwin = sem("general_window")
        s_gadd = sem("general_added")
        s_gstep = sem("general_steps")

        x_view = x.rearrange("(c b p) f -> c p b f", p=NB, b=BPG)
        out_view = out.rearrange("(c b p) f -> c p b f", p=NB, b=BPG)
        table_view = table.rearrange("(c b p) f -> c p b f", p=NB, b=BPG)
        rec_view = records.rearrange("(k r) w -> k r w", r=ROWS)

        def blocks(ap):
            return ap.rearrange("p (b f) -> p b f", b=BPG)

        def apart(eng):
            eng.sem_inc(s_apart, 1)

        def flat_free(a):
            return a[:, :, :].rearrange("p b t -> p (b t)")

        def flat(a):
            return a.rearrange("(o n) -> o n", o=1)

        def attr_of(k):
            if isinstance(k, int) and k == CHUNKS - 1:
                a = attr[TAIL0:EDGES, :]
            else:
                a = attr[bass.ds(k * CE, CE), :]
            return a.rearrange("(p t) f -> p t f", t=EPP)

        blk = ctx.enter_context(nc.Block())

        @blk.sync
        def _(sp):
            for rows, e in ((dst_i, dst), (src_i, src)):
                last = (CHUNKS - 1) * EPP
                sp.dma_start(rows[:, 0:last].rearrange("p (k t) -> p k t", t=EPP),
                             e[0:(CHUNKS - 1) * CE].rearrange("(k p t) -> p k t", p=P, t=EPP)).then_inc(s_ends, 16)
                sp.dma_start(rows[:, last:EC], e[TAIL0:EDGES].rearrange("(p t) -> p t", t=EPP)).then_inc(s_ends, 16)
            for n in range(2):
                sp.dma_start(rec[n][:, :, 0:FEATS], attr_of(n)).then_inc(s_attr[n], 16)
            for c in range(GROUPS):
                sp.dma_start(blocks(x_rows[:, c, :]), x_view[c]).then_inc(s_x, 16)
            sp.dma_start(be_all[:, :], flat(be).to_broadcast((NB, HID))).then_inc(s_x, 16)
            sp.dma_start(we_f[:, :], we).then_inc(s_we, 16)
            for n in range(STACK // FEATS):
                sp.dma_start(we_rows[n * FEATS:(n + 1) * FEATS, 0, :], we).then_inc(s_we, 16)
            sp.wait_ge(s_zero, 1)
            for n, (lo, hi) in enumerate(((0, 2), (2, CHUNKS))):
                sp.dma_start(rec_view[lo:hi, 0:SORT_SLOTS, :].rearrange("k (p j) w -> p k (j w)", p=P),
                             zeros[:, :].unsqueeze(1).to_broadcast((P, hi - lo, FILLED * REC))).then_inc(s_cleared[n], 16)
            sp.dma_start(w12[:, :].rearrange("p (l n) -> p l n", l=LAYERS)[:, :, 0:HID], w1.rearrange("l k n -> k l n")).then_inc(s_par, 16)
            sp.dma_start(w12[:, :].rearrange("p (l n) -> p l n", l=LAYERS)[:, :, HID:2 * HID], w2.rearrange("l k n -> k l n")).then_inc(s_par, 16)
            with nc.allow_non_contiguous_dma(reason="512 biases, once"):
                sp.dma_start(b1_cols[:, :], b1.rearrange("l n -> n l")).then_inc(s_par, 16)
            sp.dma_start(b2_rows[:, :], b2.rearrange("(o l) n -> o (l n)", o=1).to_broadcast((3, LAYERS * HID))).then_inc(s_par, 16)
            for rows, par in ((g_all, ln_g), (b_all, ln_b)):
                sp.dma_start(rows[:, :], par.rearrange("(o l) n -> o (l n)", o=1).to_broadcast((NB, LAYERS * HID))).then_inc(s_par, 16)

            def store_table(first):
                for c in range(GROUPS):
                    sp.wait_ge(s_tab, first + c + 1)
                    sp.dma_start(table_view[c], blocks(tab_rows[:, c, :])).then_inc(s_table, 16)

            store_table(0)

            def read_slots(k, s, use):
                sp.wait_ge(s_slotfree, k + 1)
                sp.wait_ge(s_attr[s], use * 16)
                sp.wait_ge(s_row, k + 1)
                sp.dma_start(slots[:, FILLED:TILES, :], rec[s][:, SORTED:EPP, :]).then_inc(s_slot, 16)
                sp.wait_ge(s_scat[s], use * (16 * SORTED))
                sp.dma_start(slots[:, 0:FILLED, :].rearrange("p j w -> p (j w)"),
                             rec_view[bass.ds(k, 1), 0:SORT_SLOTS, :].rearrange("o (p j) w -> p (o j w)", p=P)).then_inc(s_slot, 16)

            with sp.Fori(0, PAIRS - 2) as i:
                for s in range(2):
                    read_slots(i * 2 + s, s, i + 1)
                    sp.wait_ge(s_slot, (i * 2 + s + 1) * 32)
                    sp.dma_start(rec[s][:, :, 0:FEATS], attr_of(i * 2 + s + 2)).then_inc(s_attr[s], 16)
            for s in range(2):
                read_slots(CHUNKS - 4 + s, s, PAIRS - 1)
                sp.wait_ge(s_slot, (CHUNKS - 3 + s) * 32)
                sp.dma_start(rec[s][:, :, 0:FEATS], attr_of(CHUNKS - 2 + s)).then_inc(s_attr[s], 16)
            for s in range(2):
                read_slots(CHUNKS - 2 + s, s, PAIRS)

            sp.wait_ge(s_saved, 32 * CHUNKS)
            sp.wait_ge(s_flag, 1)
            flag = sp.value_load(flag_i[0:1, 0:1])

            def load_chunk(l, k, s):
                sp.wait_ge(s_sum, ((l + 1) * CHUNKS + k - 1) * BATCHES)
                sp.dma_start(stack_now[s][:, :], stacks[bass.ds(k, 1)].rearrange("o a b -> (o a) b")).then_inc(s_str[s], 16)
                sp.dma_start(pick_now[s][:, :].bitcast(U8), picks[bass.ds(k, 1)].rearrange("o a b -> (o a) b")).then_inc(s_str[s], 16)

            with sp.Fori(0, LAYERS) as l:
                with sp.If(l < LAYERS - 1):
                    for s in range(2):
                        load_chunk(l, s, s)
                with sp.If(0 < flag):
                    with sp.Fori(0, CHUNKS - 1) as k:
                        sp.wait_ge(s_gfree, l * CHUNKS + k + 1)
                        sp.dma_start(g_attr.rearrange("p (t f) -> p t f", f=FEATS), attr_of(k)).then_inc(s_gattr, 16)
                    sp.wait_ge(s_gfree, (l + 1) * CHUNKS)
                    sp.dma_start(g_attr.rearrange("p (t f) -> p t f", f=FEATS), attr_of(CHUNKS - 1)).then_inc(s_gattr, 16)
                store_table((l + 1) * GROUPS)
                with sp.If(l < LAYERS - 1):
                    with sp.Fori(1, PAIRS) as i:
                        for s in range(2):
                            load_chunk(l, i * 2 + s, s)
            for c in range(GROUPS):
                sp.wait_ge(s_norm, LAYERS * GROUPS + c + 1)
                sp.dma_start(out_view[c], blocks(x_rows[:, c, :])).then_inc(s_out, 16)
            sp.wait_ge(s_table, 16 * GROUPS * (LAYERS + 1))
            sp.wait_ge(s_out, 16 * GROUPS)

        @blk.gpsimd
        def _(pool):
            G = nc.gpsimd
            G.memset(zeros[:, :], 0.0).then_inc(s_zero, 1)
            G.iota(iota_i[:, :], pattern=[[1, P]], base=0, channel_multiplier=0)
            G.iota(part_i[:, :], pattern=[[0, 1]], base=0, channel_multiplier=1)
            G.iota(base_i, pattern=[[ROWS, CHUNKS], [0, EPP]], base=0, channel_multiplier=0)
            G.iota(lost_i[:, :], pattern=[[P, SORTED]], base=0, channel_multiplier=1)
            G.memset(ident[:, :], 0.0)
            G.memset(ones[:, :], 1.0).then_inc(s_const, 1)
            pool.wait_ge(s_const, 1)
            G.affine_select(out=ident[:, :], in_=ident[:, :], compare_op=ALU.not_equal, fill=1.0,
                            base=0, pattern=[[-1, P]], channel_multiplier=1)
            G.affine_select(out=before_f[:, :], in_=ones[:, :], compare_op=ALU.is_gt, fill=0.0,
                            base=0, pattern=[[1, P]], channel_multiplier=-1).then_inc(s_const, 1)
            last = slice((CHUNKS - 1) * EPP, EC)

            def mask(ap, fill):
                return G.affine_select(out=ap, in_=ap, compare_op=ALU.is_ge, fill=fill,
                                       base=-OVERLAP, pattern=[[1, EPP]], channel_multiplier=EPP)

            pool.wait_ge(s_masked, 1)
            mask(meta[:, last, 1], 0.0)
            mask(dst_f[:, last], NOWHERE).then_inc(s_masked, 1)
            pool.wait_ge(s_cleared[0], 16)

            def scatter_records(s, tiles):
                for t in tiles:
                    G.indirect_dma_start(out=records, out_offset=bass.IndirectOffsetOnAxis(ap=row_i[s][:, t:t + 1], axis=0),
                                         in_=rec[s][:, t, :], in_offset=None).then_inc(s_scat[s], 16)

            def records_there(k, s, use):
                pool.wait_ge(s_attr[s], use * 16)
                pool.wait_ge(s_row, k + 1)
                apart(pool)

            def scatter_and_gather(k, s, use, use_before):
                records_there(k, s, use)
                scatter_records(s, range(0, FIRST_PART))
                pool.wait_ge(s_table, 16 * GROUPS)
                gather_spare(1 - s, use_before)
                scatter_records(s, range(FIRST_PART, SORTED))

            def gather_spare(s, use):
                pool.wait_ge(s_staged[s], use)
                apart(pool)
                for t in range(FETCHED):
                    G.indirect_dma_start(out=gath[s][:, t * HID:(t + 1) * HID], out_offset=None, in_=table,
                                         in_offset=bass.IndirectOffsetOnAxis(ap=spare_now[s][:, t:t + 1], axis=0),
                                         ).then_inc(s_gath[s], 16)

            records_there(0, 0, 1)
            scatter_records(0, range(SORTED))
            pool.wait_ge(s_masked, 3)
            mask(block_f[:, last], NO_BLOCK).then_inc(s_masked, 1)
            pool.wait_ge(s_cleared[1], 16)
            with pool.Fori(0, PAIRS - 1) as i:
                scatter_and_gather(i * 2 + 1, 1, i + 1, i + 1)
                scatter_and_gather(i * 2 + 2, 0, i + 2, i + 1)
            scatter_and_gather(CHUNKS - 1, 1, PAIRS, PAIRS)
            gather_spare(1, PAIRS)

            pool.wait_ge(s_flag, 1)
            flag = pool.value_load(flag_i[0:1, 0:1])
            with pool.Fori(0, LAYERS) as l:
                with pool.If(0 < flag):
                    with pool.Fori(0, EC) as n:
                        pool.wait_ge(s_gtile, l * EC + n + 1)
                        apart(pool)
                        G.indirect_dma_start(out=g_rows, out_offset=None, in_=table,
                                             in_offset=bass.IndirectOffsetOnAxis(ap=g_src[:, 0:1], axis=0)).then_inc(s_ggath, 16)
                n = (l + 1) * GROUPS
                for c in range(GROUPS + 2):
                    if c < GROUPS:
                        pool.wait_ge(s_h, n + c - GROUPS + 1)
                        G.tensor_tensor(out=tab_rows[:, c, :], in0=h_rows[:, c, :], in1=be_wide[:, :], op=ALU.add).then_inc(s_tab, 1)
                    if 1 <= c <= GROUPS:
                        cols = slice((c - 1) * GF, c * GF)
                        pool.wait_ge(s_parts, n + max(c - 2, 0))
                        pool.wait_ge(s_part1, n - GROUPS + c)
                        G.tensor_tensor(out=rest[c % 2][:, :], in0=tab_rows[:, c - 1, :], in1=parts[:, 0, cols], op=ALU.subtract).then_inc(s_rest, 1)
                    if c >= 2:
                        cols = slice((c - 2) * GF, (c - 1) * GF)
                        pool.wait_ge(s_part2, n - GROUPS + c - 1)
                        G.tensor_tensor(out=parts[:, 2, cols], in0=rest[(c - 1) % 2][:, :], in1=parts[:, 1, cols], op=ALU.subtract).then_inc(s_parts, 1)
                with pool.If(l < LAYERS - 1):
                    pool.wait_ge(s_table, (l + 2) * (16 * GROUPS))
                    apart(pool)
                    with pool.Fori(0, PAIRS) as i:
                        for s in range(2):
                            gather_spare(s, (l + 1) * PAIRS + i + 1)

        def start_sums(act, c, count):
            act.wait_ge(s_htr, count)
            nc.scalar.copy(z_cols[:, c * GN:(c + 1) * GN].rearrange("p (b n) -> p b n", b=BPG),
                           blocks(p_tr[:, 0:GF])[:, :, 0:NB]).then_inc(s_zc, 1)

        @blk.scalar
        def _(act):
            S = nc.scalar
            act.wait_ge(s_x, 16 * (GROUPS + 1))
            S.copy(h_rows[:, :, :], x_rows[:, :, :]).then_inc(s_h0, 1)
            for c in range(GROUPS):
                start_sums(act, c, c + 1)

            def relu_batches(c, last_step):
                for b in range(ACT_BATCHES):
                    act.wait_ge(s_sc, c * BATCHES + b + 1)
                    act.wait_ge(s_sum, c * BATCHES + b + 1)
                    S.activation(msg[b % RING][:, :], bank(b % RING), ACT.Relu).then_inc(s_act, 1)
                    if b == 1:
                        last_step()

            def save_chunk(k, s):
                for b in range(4):
                    act.wait_ge(s_strp, k * 4 + b + 1)
                    lo, hi = b * 8, min(b * 8 + 8, TILES)
                    S.copy(stack_now[s][:, lo * P:hi * P], bank(2 + b % 2).bitcast(BF16)[0:STACK, 0:(hi - lo) * P]).then_inc(s_stc, 1)
                act.wait_ge(s_stc, (k + 1) * 4)
                act.dma_start(stacks[bass.ds(k, 1)].rearrange("o a b -> (o a) b"), stack_now[s][:, :]).then_inc(s_saved, 16)
                act.wait_ge(s_pick, (k + 1) * 7)
                act.dma_start(picks[bass.ds(k, 1)].rearrange("o a b -> (o a) b"), pick_now[s][:, :].bitcast(U8)).then_inc(s_saved, 16)

            with act.Fori(0, PAIRS) as i:
                for s in range(2):
                    k = i * 2 + s
                    save_chunk(k, s)
                    relu_batches(k, lambda: None)
                    act.wait_ge(s_saved, (k + 1) * 32)
                    act.sem_inc(s_savefree, 1)

            act.wait_ge(s_flag, 1)
            act.wait_ge(s_par, 16 * 6)

            def stage(k, s):
                S.copy(spare_now[s][:, :], spare_src[:, bass.ds(k * FETCHED, FETCHED)]).then_inc(s_staged[s], 1)

            def deviation(c, count):
                act.wait_ge(s_var, count)
                S.activation(std[c % 2][:, :], mv[c % 2][:, :, 1], ACT.Sqrt, bias=eps[:, 0:1]).then_inc(s_std, 1)

            def normalize(c, count, z, to):
                act.wait_ge(s_scale, count)
                for b in range(BPG):
                    row = slice(b * HID, (b + 1) * HID)
                    last = S.activation(to[:, row], z[:, row], ACT.Identity, bias=shift[c % 2][:, b:b + 1], scale=rstd[c % 2][:, b:b + 1])
                last.then_inc(s_norm, 1)

            stage(0, 0)
            with act.Fori(0, LAYERS) as l:
                S.copy(w_now[:, :], w12[:, bass.ds(l * (2 * HID), 2 * HID)]).then_inc(s_wnow, 1)
                n = l * GROUPS

                S.activation(root_ready[:, :], eps[:, :], ACT.Sqrt)

                def hidden_relu(c):
                    act.wait_ge(s_hidp, n + c + 1)
                    if c:
                        act.wait_ge(s_z2p, n + c)
                    apart(act)
                    bias = b1_cols[:, bass.ds(l, 1)]
                    S.activation(hid[:, 0:GA], p_hid[:, 0:GA], ACT.Relu, bias=bias)
                    S.activation(hid[:, GA:GN], p_hid[:, 512:512 + GB], ACT.Relu, bias=bias).then_inc(s_hid, 1)

                hidden_relu(0)
                for c in range(GROUPS + 2):
                    if c + 1 < GROUPS:
                        hidden_relu(c + 1)
                    if c < GROUPS:
                        deviation(c, n + c + 1)
                        if c >= 2:
                            act.wait_ge(s_h, n + c - 1)
                        normalize(c, n + c + 1, p_z2[c % 2][0:NB, 0:GF], zn[c % 2])
                    if 1 <= c <= GROUPS:
                        cols = slice((c - 1) * GF, c * GF)
                        act.wait_ge(s_tab, n + GROUPS + c)
                        S.copy(parts[:, 0, cols], tab_rows[:, c - 1, :]).then_inc(s_part1, 1)
                    if c >= 2:
                        start_sums(act, c - 2, n + GROUPS + c - 1)
                        cols = slice((c - 2) * GF, (c - 1) * GF)
                        act.wait_ge(s_rest, n + c - 1)
                        S.copy(parts[:, 1, cols], rest[(c - 1) % 2][:, :]).then_inc(s_part2, 1)
                with act.If(l < LAYERS - 1):
                    with act.Fori(0, PAIRS) as i:
                        for s in range(2):
                            k = i * 2 + s
                            c = (l + 1) * CHUNKS + k

                            def next_rows():
                                act.wait_ge(s_left, c * 2 + 1)
                                apart(act)
                                stage(k + 1, 1 - s)

                            relu_batches(c, next_rows)
            for c in range(GROUPS):
                count = LAYERS * GROUPS + c + 1
                deviation(c, count)
                normalize(c, count, zn[c % 2], x_rows[:, c, :])

        @blk.vector
        def _(dve):
            V = nc.vector
            TT = V.tensor_tensor
            prep = Chain(dve, s_prep)
            V.memset(eps[:, :], EPS)
            V.memset(z_cols[:, NODES:ZW], 0.0)
            V.memset(goes_on[:, :, 1:SORTED], 1.0)
            V.memset(goes_on[:, :, 0:1], 0.0)
            V.memset(most[:, :], 0.0)
            V.memset(block_all[:, EC:], NO_BLOCK)
            dve.sem_inc(s_slotfree, 1)
            dve.sem_inc(s_savefree, 2)
            dve.sem_inc(s_left, 1)
            dve.sem_inc(s_added, 2)
            dve.sem_inc(s_gfree, 1)
            dve.sem_inc(s_gz, 1)
            dve.wait_ge(s_const, 2)
            V.tensor_copy(iota_f[:, :], iota_i[:, :])
            V.tensor_copy(part_f[:, :], part_i[:, :])
            V.tensor_copy(base_f[:, :], tmp_i[:, :])
            V.tensor_copy(ident_b[:, :], ident[:, :])
            V.tensor_copy(lost_f[:, :], lost_i[:, :])
            prep(V.tensor_copy(before[:, :], before_f[:, :]))
            V.memset(meta[:, :, 3], 0.0)
            dve.wait_ge(s_ends, 64)
            prep(V.tensor_copy(dst_f[:, :], dst_i[:, :]))
            by_chunk = lambda a: a.rearrange("p (k t) -> p k t", t=EPP)
            V.tensor_reduce(ends[:, 0, :], by_chunk(dst_f[:, :]), axis=AX.X, op=ALU.min)
            prep(V.tensor_reduce(ends[:, 1, :], by_chunk(dst_f[:, :]), axis=AX.X, op=ALU.max))
            dve.wait_ge(s_prep_pe, 1)
            V.tensor_reduce(span[:, 0:1], bank(0)[0:CHUNKS, 0:P], axis=AX.X, op=ALU.min)
            prep(V.tensor_reduce(span[:, 1:2], bank(0)[0:CHUNKS, P:2 * P], axis=AX.X, op=ALU.max))
            prep(TT(out=span[:, 2:3], in0=span[:, 1:2], in1=span[:, 0:1], op=ALU.subtract))
            dve.wait_ge(s_prep_pe, 2)
            V.tensor_copy(first_i[:, :], bank(1)[0:1, 0:CHUNKS])
            prep(V.tensor_copy(first_row[:, :], bank(1)[0:1, 0:2 * CHUNKS]))
            dve.wait_ge(s_prep_pe, 3)
            prep(V.tensor_copy(first_all[:, :], bank(0)[:, 0:CHUNKS]))
            prep(V.scalar_tensor_tensor(out=meta[:, :, 1].rearrange("p (k t) -> p k t", t=EPP), in0=by_chunk(dst_f[:, :]), scalar=1.0,
                                        in1=first_all[:, :].unsqueeze(2).to_broadcast((P, CHUNKS, EPP)), op0=ALU.add, op1=ALU.subtract))
            dve.sem_inc(s_masked, 1)

            def sources(e):
                a, b, block = tmp_a[:, e], tmp_b[:, e], block_f[:, e]
                V.tensor_copy(meta[:, e, 2].bitcast(I32), src_i[:, e])
                prep(V.tensor_copy(a, src_i[:, e]))
                prep(V.tensor_scalar(tmp_i[:, e], a, 1.0 / NB, 0.5 / NB - 0.5, ALU.mult, ALU.add))
                prep(V.tensor_copy(block, tmp_i[:, e]))
                prep(V.scalar_tensor_tensor(out=a, in0=block, scalar=-float(NB), in1=a, op0=ALU.mult, op1=ALU.add))
                prep(V.tensor_scalar(b, a, 0.0, None, ALU.is_lt))
                prep(V.scalar_tensor_tensor(out=b, in0=a, scalar=float(NB), in1=b, op0=ALU.is_ge, op1=ALU.subtract))
                prep(TT(out=block, in0=block, in1=b, op=ALU.add))
                prep(V.scalar_tensor_tensor(out=a, in0=b, scalar=-float(NB), in1=a, op0=ALU.mult, op1=ALU.add))
                prep(V.tensor_scalar(meta[:, e, 0], a, 1.0, None, ALU.add))

            sources(slice(0, 2 * EPP))

            OWN_STEPS, RANK_STEPS = 2, 15
            rank = Chain(dve, s_rank)

            def rank_own(k):
                rank.at(k * RANK_STEPS)
                rank(TT(out=own[:, :, :], in0=block_all[:, bass.ds(k * EPP, SORTED)].unsqueeze(1).to_broadcast((P, BLOCKS, SORTED)),
                        in1=iota_f[:, 0:BLOCKS].unsqueeze(2).to_broadcast((P, BLOCKS, SORTED)), op=ALU.is_equal))
                rank(V.tensor_tensor_scan(flat_free(run), flat_free(goes_on), flat_free(own), 0.0, ALU.mult, ALU.add))
                dve.sem_inc(s_tot, 1)

            def rank_blocks(k):
                rank.at(k * RANK_STEPS + OWN_STEPS)
                dve.wait_ge(s_pre, 2 * k + 1)
                rank(TT(out=rank_w[:, :, :], in0=run[:, :, :], in1=p_before[0][:, 0:BLOCKS].unsqueeze(2).to_broadcast((P, BLOCKS, SORTED)), op=ALU.add))
                rank(TT(out=rank_w[:, :, :], in0=rank_w[:, :, :], in1=own[:, :, :], op=ALU.mult))

            def rank_over(k):
                rank(V.tensor_reduce(rank1[:, :], rank_w[:, :, :].rearrange("p b t -> p t b"), axis=AX.X, op=ALU.add))
                rank(V.tensor_scalar(over[:, :], rank1[:, :], float(P + 1), None, ALU.is_ge))
                rank(V.tensor_tensor_scan(over_run[:, :], ones[:, 0:SORTED], over[:, :], 0.0, ALU.mult, ALU.add))
                dve.sem_inc(s_tot, 1)

            def rank_rows(k, s):
                edges = bass.ds(k * EPP, SORTED)
                dve.wait_ge(s_pre, 2 * k + 2)
                V.tensor_scalar(tile_f[:, :], block_f[:, edges], -1.0, float(BLOCKS), ALU.mult, ALU.add)
                rank(V.scalar_tensor_tensor(out=rr[:, :], in0=over_run[:, :], scalar=p_before[1][:, 0:1], in1=rank1[:, :], op0=ALU.add, op1=ALU.subtract))
                TT(out=tile_f[:, :], in0=tile_f[:, :], in1=over[:, :], op=ALU.mult)
                rank(TT(out=rr[:, :], in0=rr[:, :], in1=over[:, :], op=ALU.mult))
                TT(out=tile_f[:, :], in0=tile_f[:, :], in1=block_f[:, edges], op=ALU.add)
                rank(TT(out=rr[:, :], in0=rr[:, :], in1=rank1[:, :], op=ALU.add))
                TT(out=most[:, :], in0=most[:, :], in1=rr[:, :], op=ALU.max)
                V.tensor_scalar(bad_f[:, :], rr[:, :], float(P + 1), None, ALU.is_ge)
                rank(V.scalar_tensor_tensor(out=row_f[:, :], in0=rr[:, :], scalar=float(FILLED), in1=tile_f[:, :], op0=ALU.mult, op1=ALU.add))
                V.scalar_tensor_tensor(out=bad_f[:, :], in0=rank1[:, :], scalar=1.0, in1=bad_f[:, :], op0=ALU.is_lt, op1=ALU.add)
                rank(V.tensor_scalar(up[:, :], row_f[:, :], -1.0, float(SORT_SLOTS + FILLED), ALU.mult, ALU.add))
                V.tensor_scalar(row_f[:, :], row_f[:, :], -float(FILLED), None, ALU.add)
                rank(TT(out=up[:, :], in0=up[:, :], in1=lost_f[:, :], op=ALU.add))
                rank(TT(out=up[:, :], in0=up[:, :], in1=bad_f[:, :], op=ALU.mult))
                rank(TT(out=row_f[:, :], in0=row_f[:, :], in1=up[:, :], op=ALU.add))
                V.tensor_copy(rec[s][:, :, FEATS:REC].bitcast(I32), meta[:, bass.ds(k * EPP, EPP), :].bitcast(I32))
                TT(out=row_i[s][:, :], in0=row_f[:, :], in1=base_f[:, edges], op=ALU.add).then_inc(s_row, 1)
                assert rank.n == RANK_STEPS - OWN_STEPS

            UNPACK_STEPS = 4
            unp = Chain(dve, s_unp)

            def unpack_chunk(k, s):
                unp.at(k * UNPACK_STEPS)
                stack = lambda n, m=1: stack_rows[:, :, n * FEATS:(n + m) * FEATS]
                feat = slots[:, :, 0:FEATS]
                dve.wait_ge(s_savefree, k + 1)
                dve.wait_ge(s_slot, (k + 1) * 32)
                apart(dve)
                V.tensor_copy(local_b[:, :], slots[:, 0:BLOCKS, FEATS]).then_inc(s_local, 1)
                V.tensor_copy(spare_now[s][:, :], slots[:, BLOCKS:TILES, FEATS + 2].bitcast(I32)).then_inc(s_staged[s], 1)
                unp(V.tensor_copy(stack(0), feat))
                unp(TT(out=a_left[:, :, :], in0=feat, in1=stack(0), op=ALU.subtract))
                V.tensor_copy(stack(1), stack(0))
                V.tensor_copy(stack(2), stack(0))
                unp(V.tensor_copy(stack(3), a_left[:, :, :]))
                V.tensor_copy(stack(4), stack(3))
                unp(TT(out=stack(5), in0=a_left[:, :, :], in1=stack(3), op=ALU.subtract))
                dve.sem_inc(s_stackrows, 1)
                V.tensor_copy(targets[:, bass.ds(k * TILES, TILES)], slots[:, :, FEATS + 1])
                V.tensor_copy(spare_src[:, bass.ds(k * FETCHED, FETCHED)], slots[:, BLOCKS:TILES, FEATS + 2].bitcast(I32)).then_inc(s_slotfree, 1)
                for b in range(7):
                    lo, hi = b * 4 * P, min(b * 4 + 4, BLOCKS) * P
                    dve.wait_ge(s_bc, k * 7 + b + 1)
                    apart(dve)
                    V.tensor_scalar(pick_now[s][:, lo:hi], bank(4 + b % 2)[0:NB, 0:hi - lo], part1[0:NB, 0:1], None, ALU.is_equal,
                                    saturate=False).then_inc(s_pick, 1)
                assert unp.n == UNPACK_STEPS

            V.tensor_scalar(iota1[:, :], iota_f[:, :], 1.0, None, ALU.add)
            prep(V.tensor_scalar(part1[:, :], part_f[:, :], 1.0, None, ALU.add))
            for k in range(2):
                rank_own(k)
                rank_blocks(k)
                rank_over(k)
                rank_rows(k, k)
            sources(slice(2 * EPP, EC))
            dve.sem_inc(s_masked, 1)
            dve.wait_ge(s_we, 16 * (1 + STACK // FEATS))
            wr = we_rows
            prep(V.tensor_copy(we_stack[:, :], wr[:, 0, :]))
            prep(V.tensor_copy(wr[:, 1, :], we_stack[:, :]))
            prep(TT(out=wr[:, 3, :], in0=wr[:, 0, :], in1=wr[:, 1, :], op=ALU.subtract))
            prep(V.tensor_copy(we_stack[:, :], wr[:, 3, :]))
            prep(V.tensor_copy(wr[:, 2, :], we_stack[:, :]))
            prep(TT(out=wr[:, 3, :], in0=wr[:, 3, :], in1=wr[:, 2, :], op=ALU.subtract))
            for part in range(3):
                V.memset(part_sel[:, part:part + 1], 0.0)
            prep(V.tensor_scalar(part_sel[:, 3:4], part_f[0:STACK, :], 0.0, None, ALU.mult))
            for part, rows in enumerate(((0, 3, 5), (1, 4), (2,))):
                for r in rows:
                    prep(V.tensor_scalar(part_sel[:, 3:4], part_f[0:STACK, :], float(r * FEATS), None, ALU.is_ge))
                    prep(V.scalar_tensor_tensor(out=part_sel[:, 3:4], in0=part_f[0:STACK, :], scalar=float((r + 1) * FEATS),
                                                in1=part_sel[:, 3:4], op0=ALU.is_lt, op1=ALU.mult))
                    prep(TT(out=part_sel[:, part:part + 1], in0=part_sel[:, part:part + 1], in1=part_sel[:, 3:4], op=ALU.add))
            prep(V.tensor_scalar(wr[:, 0, :], wr[:, 1, :], part_sel[:, 0:1], None, ALU.mult))
            prep(V.scalar_tensor_tensor(out=wr[:, 0, :], in0=wr[:, 2, :], scalar=part_sel[:, 1:2], in1=wr[:, 0, :], op0=ALU.mult, op1=ALU.add))
            prep(V.scalar_tensor_tensor(out=we_stack[:, :], in0=wr[:, 3, :], scalar=part_sel[:, 2:3], in1=wr[:, 0, :], op0=ALU.mult, op1=ALU.add))

            dve.wait_ge(s_x, 16 * (GROUPS + 1))
            prep(V.tensor_copy(be_wide[:, :].rearrange("p (b f) -> p b f", b=BPG), be_all[:, :].unsqueeze(1).to_broadcast((NB, BPG, HID))))
            for c in range(GROUPS):
                cols = slice(c * GF, (c + 1) * GF)
                TT(out=tab_rows[:, c, :], in0=x_rows[:, c, :], in1=be_wide[:, :], op=ALU.add).then_inc(s_tab, 1)
                dve.wait_ge(s_tab, c + 1)
                prep(V.tensor_copy(parts[:, 0, cols], tab_rows[:, c, :]))
                prep(TT(out=zn[1], in0=tab_rows[:, c, :], in1=parts[:, 0, cols], op=ALU.subtract))
                prep(V.tensor_copy(parts[:, 1, cols], zn[1]))
                TT(out=parts[:, 2, cols], in0=zn[1], in1=parts[:, 1, cols], op=ALU.subtract).then_inc(s_parts, 1)
                dve.wait_ge(s_parts, c + 1)

            def one_hot(k, c, b):
                n = min(TB, TILES - b * TB)
                dve.wait_ge(s_sc, c * BATCHES + b + 1)
                TT(out=hot[b % RING][:, 0:n, :], in0=iota1[:, :].unsqueeze(1).to_broadcast((P, n, WIN)),
                   in1=targets[:, bass.ds(k * TILES + b * TB, n)].unsqueeze(2).to_broadcast((P, n, WIN)),
                   op=ALU.is_equal).then_inc(s_hot, 1)

            def fetched(s, c, b, use):
                n = min(TB, TILES - b * TB)
                own_cols = HID * (BLOCKS - b * TB) if b == ACT_BATCHES else 0
                at = HID * (b * TB - BLOCKS) + own_cols
                dve.wait_ge(s_gath[s], use * (16 * FETCHED))
                dve.wait_ge(s_sum, c * BATCHES + b + 1)
                m = msg[b % RING]
                if own_cols:
                    V.tensor_scalar(m[:, 0:own_cols], bank(b % RING)[:, 0:own_cols], 0.0, None, ALU.max)
                TT(out=m[:, own_cols:n * HID], in0=bank(b % RING)[:, own_cols:n * HID],
                   in1=gath[s][:, at:at + n * HID - own_cols], op=ALU.add).then_inc(s_leftstep, 1)
                dve.wait_ge(s_leftstep, c * 2 + (b - ACT_BATCHES + 1))
                V.tensor_scalar(m[:, own_cols:n * HID], m[:, own_cols:n * HID], 0.0, None, ALU.max).then_inc(s_left, 1)

            def add_window(s, c, node):
                dve.wait_ge(s_sc, (c + 1) * BATCHES + RING)
                TT(out=z_cols[:, bass.ds(node, WIN)], in0=z_cols[:, bass.ds(node, WIN)], in1=p_win[s][:, 0:WIN],
                   op=ALU.add).then_inc(s_added, 1)
                dve.wait_ge(s_added, c + 3)
                apart(dve)

            def first_node(k):
                return dve.value_load(first_i[0:1, bass.ds(k, 1)], min_val=0, max_val=NODES - 1)

            def edge_chunk(k, s, c, use):
                for b in range(1, BATCHES):
                    if b == 4:
                        node = first_node(k)
                    one_hot(k, c, b)
                    if b >= ACT_BATCHES:
                        fetched(s, c, b, use)
                one_hot(k + 1, c + 1, 0)
                add_window(s, c, node)

            def parts_of_b2():
                left, high = tmp_a[0:3, 0:LAYERS * HID], tmp_b[0:3, 0:LAYERS * HID]
                V.memset(ones_b[:, :], 1.0)
                for n in range(3):
                    V.tensor_scalar(part_is[:, n:n + 1], part_f[0:3, :], float(n), None, ALU.is_equal)
                dve.wait_ge(s_par, 16 * 6)
                prep(V.tensor_copy(b2_parts[:, :], b2_rows[:, :]))
                prep(V.tensor_copy(high, b2_parts[:, :]))
                prep(TT(out=left, in0=b2_rows[:, :], in1=high, op=ALU.subtract))
                V.tensor_scalar(b2_rows[:, :], high, part_is[:, 0:1], None, ALU.mult)
                prep(V.tensor_copy(b2_parts[:, :], left))
                prep(V.tensor_copy(high, b2_parts[:, :]))
                prep(TT(out=left, in0=left, in1=high, op=ALU.subtract))
                prep(V.scalar_tensor_tensor(out=b2_rows[:, :], in0=high, scalar=part_is[:, 1:2], in1=b2_rows[:, :], op0=ALU.mult, op1=ALU.add))
                prep(V.scalar_tensor_tensor(out=b2_parts[:, :], in0=left, scalar=part_is[:, 2:3], in1=b2_rows[:, :], op0=ALU.mult, op1=ALU.add))

            dve.wait_ge(s_zc, GROUPS)
            dve.wait_ge(s_masked, 4)
            dve.wait_ge(s_h0, 1)
            rank_own(2)
            with dve.Fori(0, PAIRS - 1) as i:
                for s in range(2):
                    k = i * 2 + s
                    unpack_chunk(k, s)
                    one_hot(k, k, 0)
                    rank_blocks(k + 2)
                    rank_over(k + 2)
                    one_hot(k, k, 1)
                    rank_rows(k + 2, s)
                    for b in range(2, BATCHES):
                        if b == 4:
                            node = first_node(k)
                        if b == 5:
                            rank_own(k + 3)
                        one_hot(k, k, b)
                        if b >= ACT_BATCHES:
                            fetched(s, k, b, i + 1)
                    add_window(s, k, node)
            for s in range(2):
                k = CHUNKS - 2 + s
                node = first_node(k)
                unpack_chunk(k, s)
                for b in range(BATCHES):
                    if s == 0 and b == ACT_BATCHES:
                        parts_of_b2()
                    one_hot(k, k, b)
                    if b >= ACT_BATCHES:
                        fetched(s, k, b, PAIRS)
                add_window(s, k, node)
            V.tensor_copy(targets[:, CHUNKS * TILES:], targets[:, 0:TB]).then_inc(s_again, 1)
            dve.wait_ge(s_again, 1)
            one_hot(0, CHUNKS, 0)

            V.tensor_reduce(most1[:, :], most[:, :], axis=AX.X, op=ALU.max).then_inc(s_tot, 1)
            dve.wait_ge(s_slotfree, CHUNKS + 1)
            V.tensor_copy(spare_src[:, CHUNKS * FETCHED:], spare_src[:, 0:FETCHED])
            dve.wait_ge(s_prep_pe, 4)
            V.tensor_reduce(flag_f[:, 0:1], first_row[0:1, CHUNKS:2 * CHUNKS], axis=AX.X, op=ALU.max)
            prep(V.tensor_reduce(flag_f[:, 1:2], bank(0)[0:1, 0:P], axis=AX.X, op=ALU.max))
            prep(V.tensor_scalar(flag_f[:, 0:1], flag_f[:, 0:1], float(WIN), None, ALU.is_ge))
            prep(V.tensor_scalar(flag_f[:, 1:2], flag_f[:, 1:2], float(SPARE * P + 1), None, ALU.is_ge))
            TT(out=flag_i[:, :], in0=flag_f[:, 0:1], in1=flag_f[:, 1:2], op=ALU.add).then_inc(s_flag, 1)

            dve.wait_ge(s_flag, 1)
            flag = dve.value_load(flag_i[0:1, 0:1])
            upd = Chain(dve, s_upd)
            UPD_STEPS = 4

            def by_layer(ap, l):
                return ap[:, bass.ds(l * HID, HID)].unsqueeze(1).to_broadcast((NB, BPG, HID))

            def statistics(z, c):
                for b in range(BPG):
                    last = V.bn_stats(stats[:, b, :], z[:, b * HID:(b + 1) * HID])
                upd(last)
                apart(dve)
                for b in range(BPG):
                    last = V.bn_aggr(mv[c % 2][:, b, :], stats[:, b, :])
                last.then_inc(s_var, 1)

            def scale(c, count):
                dve.wait_ge(s_std, count)
                upd(V.reciprocal(rstd[c % 2][:, :], std[c % 2][:, :]))
                V.scalar_tensor_tensor(out=shift[c % 2][:, :], in0=mv[c % 2][:, :, 0], scalar=-1.0, in1=rstd[c % 2][:, :],
                                       op0=ALU.mult, op1=ALU.mult).then_inc(s_scale, 1)

            with dve.Fori(0, LAYERS) as l:
                with dve.If(0 < flag):
                    for c in range(GROUPS):
                        dve.wait_ge(s_gtrh, l * GROUPS + c + 1)
                        V.tensor_copy(z_cols[:, c * GN:(c + 1) * GN].rearrange("p (b n) -> p b n", b=BPG),
                                      blocks(p_tr[:, 0:GF])[:, :, 0:NB]).then_inc(s_gz, 1)
                    gen = Chain(dve, s_gstep)

                    with dve.Fori(0, CHUNKS) as k:
                        dve.wait_ge(s_gattr, (l * CHUNKS + k + 1) * 16)
                        apart(dve)
                        with dve.Fori(0, EPP) as t:
                            n = l * EC + k * EPP + t
                            gen.at(n)
                            at = k * EPP + t
                            V.tensor_copy(g_feat[:, :], g_attr[:, bass.ds(t * FEATS, FEATS)])
                            V.tensor_copy(g_dst[:, :], dst_f[:, bass.ds(at, 1)])
                            V.tensor_copy(g_src[:, :], src_i[:, bass.ds(at, 1)]).then_inc(s_gtile, 1)
                            dve.wait_ge(s_gtr, n + 1)
                            V.tensor_copy(g_cols[:, :], bank(0)[0:FEATS, 0:P]).then_inc(s_gcols, 1)
                            dve.wait_ge(s_ggath, (n + 1) * 16)
                            dve.wait_ge(s_gterm, n + 1)
                            gen(TT(out=g_msg, in0=g_rows, in1=bank(1)[:, 0:HID], op=ALU.add))
                            V.tensor_scalar(g_msg, g_msg, 0.0, None, ALU.max).then_inc(s_gmsg, 1)
                            with dve.Fori(0, WINDOWS) as w:
                                m = n * WINDOWS + w
                                V.tensor_scalar(g_hot, iota_f[:, :], g_dst[:, 0:1], None, ALU.is_equal).then_inc(s_ghot, 1)
                                dve.wait_ge(s_gwin, m + 1)
                                V.tensor_scalar(g_dst[:, :], g_dst[:, :], -float(WIN), None, ALU.add)
                                TT(out=z_cols[:, bass.ds(w * WIN, WIN)], in0=z_cols[:, bass.ds(w * WIN, WIN)], in1=p_win[0][:, 0:WIN],
                                   op=ALU.add).then_inc(s_gadd, 1)
                                dve.wait_ge(s_gadd, m + 1)
                                apart(dve)
                        dve.sem_inc(s_gfree, 1)

                n = l * GROUPS
                upd.at(n * UPD_STEPS)
                for c in range(GROUPS + 1):
                    if c < GROUPS:
                        dve.wait_ge(s_z2p, n + c + 1)
                        statistics(p_z2[c % 2][0:NB, 0:GF], c)
                    if c:
                        z = zn[(c - 1) % 2]
                        dve.wait_ge(s_norm, n + c)
                        upd(TT(out=blocks(z), in0=blocks(z), in1=by_layer(g_all, l), op=ALU.mult))
                        upd(TT(out=blocks(z), in0=blocks(z), in1=by_layer(b_all, l), op=ALU.add))
                        V.scalar_tensor_tensor(out=h_rows[:, c - 1, :], in0=z, scalar=0.0, in1=h_rows[:, c - 1, :],
                                               op0=ALU.max, op1=ALU.add).then_inc(s_h, 1)
                    if c < GROUPS:
                        scale(c, n + c + 1)
                assert upd.n == GROUPS * UPD_STEPS
                with dve.If(l < LAYERS - 1):
                    dve.wait_ge(s_zc, (l + 2) * GROUPS)
                    apart(dve)
                    with dve.Fori(0, PAIRS) as i:
                        for s in range(2):
                            k = i * 2 + s
                            edge_chunk(k, s, (l + 1) * CHUNKS + k, (l + 1) * PAIRS + i + 1)
            n = LAYERS * GROUPS
            upd.at(n * UPD_STEPS)
            dve.wait_ge(s_h, n)
            for c in range(GROUPS):
                if c >= 2:
                    dve.wait_ge(s_norm, n + c - 1)
                upd(TT(out=zn[c % 2], in0=x_rows[:, c, :], in1=h_rows[:, c, :], op=ALU.add))
                statistics(zn[c % 2], c)
                scale(c, n + c + 1)

        @blk.tensor
        def _(pe):
            T = nc.tensor

            def transpose_h(rows):
                for b in range(BPG):
                    last = T.transpose(p_tr[:, b * HID:b * HID + NB], rows[:, b * HID:(b + 1) * HID], ident[0:NB, 0:NB])
                last.then_inc(s_htr, 1)

            pe.wait_ge(s_const, 2)
            pe.wait_ge(s_prep, 3)
            T.transpose(bank(0)[0:CHUNKS, 0:P], ends[:, 0, :], ident[:, :])
            T.transpose(bank(0)[0:CHUNKS, P:2 * P], ends[:, 1, :], ident[:, :]).then_inc(s_prep_pe, 1)
            pe.wait_ge(s_prep, 5)
            T.transpose(bank(1)[0:1, 0:CHUNKS], span[:, 0:1], ident[0:CHUNKS, 0:CHUNKS])
            T.transpose(bank(1)[0:1, CHUNKS:2 * CHUNKS], span[:, 2:3], ident[0:CHUNKS, 0:CHUNKS]).then_inc(s_prep_pe, 1)
            pe.wait_ge(s_prep, 6)
            T.matmul(bank(0)[:, 0:CHUNKS], ones[0:1, :], first_row[0:1, 0:CHUNKS], start=True, stop=True).then_inc(s_prep_pe, 1)
            pe.wait_ge(s_prep, 7)

            def blocks_before(k):
                pe.wait_ge(s_tot, 2 * k + 1)
                T.matmul(p_before[0][:, 0:BLOCKS], before[:, :], run[:, :, SORTED - 1], start=True, stop=True).then_inc(s_pre, 1)

            def over_before(k):
                pe.wait_ge(s_tot, 2 * k + 2)
                T.matmul(p_before[1][:, 0:1], before[:, :], over_run[:, SORTED - 1:SORTED], start=True, stop=True).then_inc(s_pre, 1)

            def unpack_products(k):
                pe.wait_ge(s_local, k + 1)
                for b in range(7):
                    if b >= 2:
                        pe.wait_ge(s_pick, k * 7 + b - 1)
                    for j in range(b * 4, min(b * 4 + 4, BLOCKS)):
                        last = T.matmul(bank(4 + b % 2)[:, (j % 4) * P:(j % 4 + 1) * P], local_b[:, j:j + 1].to_broadcast((P, P)),
                                        ident_b[:, :], start=True, stop=True)
                    last.then_inc(s_bc, 1)
                pe.wait_ge(s_stackrows, k + 1)
                for b in range(4):
                    if b >= 2:
                        pe.wait_ge(s_stc, k * 4 + b - 1)
                    for j in range(b * 8, min(b * 8 + 8, TILES)):
                        last = T.transpose(bank(2 + b % 2).bitcast(BF16)[0:STACK, (j % 8) * P:(j % 8 + 1) * P],
                                           stack_rows[:, j, :], ident_b[:, :])
                    last.then_inc(s_strp, 1)

            pe.sem_inc(s_sc, RING)

            def sums(b, s, parts_base):
                if parts_base is not None and b < ACT_BATCHES:
                    pe.wait_ge(s_parts, parts_base + min((b + 1) * TB - 1, BLOCKS - 1) // BPG + 1)
                    apart(pe)
                for j in range(b * TB, min((b + 1) * TB, TILES)):
                    to = bank(b % RING)[:, (j - b * TB) * HID:(j - b * TB + 1) * HID]
                    if j < BLOCKS:
                        for part in range(3):
                            T.matmul(to, pick_now[s][:, j * P:(j + 1) * P], parts[:, part, j * HID:(j + 1) * HID],
                                     start=(part == 0), stop=False)
                    last = T.matmul(to, stack_now[s][:, j * P:(j + 1) * P], we_stack[:, :], start=(j >= BLOCKS), stop=True)
                last.then_inc(s_sum, 1)

            def scatter(b, s, c):
                pe.wait_ge(s_hot, c * BATCHES + b + 1)
                if b < ACT_BATCHES:
                    pe.wait_ge(s_act, c * ACT_BATCHES + b + 1)
                else:
                    pe.wait_ge(s_left, c * 2 + (b - ACT_BATCHES) + 2)
                for j in range(b * TB, min((b + 1) * TB, TILES)):
                    m = j - b * TB
                    last = T.matmul(p_win[s][:, 0:WIN], msg[b % RING][:, m * HID:(m + 1) * HID], hot[b % RING][:, m, :],
                                    start=(j == 0), stop=(j == TILES - 1))
                last.then_inc(s_sc, 1)

            def edge_chunk(s, c, parts_base=None, next_loaded=None):
                for b in range(BATCHES):
                    if b + AHEAD < BATCHES:
                        sums(b + AHEAD, s, parts_base)
                    elif next_loaded is not None:
                        if b + AHEAD == BATCHES:
                            pe.wait_ge(s_str[1 - s], next_loaded)
                            apart(pe)
                        sums(b + AHEAD - BATCHES, 1 - s, None)
                    if b == 0:
                        pe.wait_ge(s_added, c + 1)
                    scatter(b, s, c)

            for k in range(2):
                blocks_before(k)
                over_before(k)
            pe.wait_ge(s_row, 2)
            pe.wait_ge(s_x, 16 * (GROUPS + 1))
            for c in range(GROUPS):
                if c:
                    pe.wait_ge(s_zc, c)
                transpose_h(x_rows[:, c, :])
            pe.wait_ge(s_zc, GROUPS)
            pe.wait_ge(s_parts, GROUPS)

            def sort_and_edge_chunk(k, s, ranked):
                if ranked is not None:
                    blocks_before(ranked)
                unpack_products(k)
                pe.wait_ge(s_stc, (k + 1) * 4)
                pe.wait_ge(s_pick, (k + 1) * 7)
                apart(pe)
                if ranked is not None:
                    over_before(ranked)
                for b in range(AHEAD):
                    sums(b, s, None)
                edge_chunk(s, k)

            with pe.Fori(0, PAIRS - 1) as i:
                for s in range(2):
                    sort_and_edge_chunk(i * 2 + s, s, i * 2 + s + 2)
            for s in range(2):
                sort_and_edge_chunk(CHUNKS - 2 + s, s, None)
            pe.wait_ge(s_tot, 2 * CHUNKS + 2)
            T.transpose(bank(0)[0:1, 0:P], most1[:, :], ident[:, :]).then_inc(s_prep_pe, 1)

            pe.wait_ge(s_flag, 1)
            flag = pe.value_load(flag_i[0:1, 0:1])

            with pe.Fori(0, LAYERS) as l:
                with pe.If(0 < flag):
                    for c in range(GROUPS):
                        pe.wait_ge(s_gz, l * GROUPS + c + 1)
                        for b in range(BPG):
                            last = T.transpose(p_tr[:, b * HID:b * HID + NB], h_rows[:, c, b * HID:(b + 1) * HID], ident[0:NB, 0:NB])
                        last.then_inc(s_gtrh, 1)
                    with pe.Fori(0, EC) as t:
                        n = l * EC + t
                        pe.wait_ge(s_gtile, n + 1)
                        T.transpose(bank(0)[0:FEATS, 0:P], g_feat[:, :], ident[:, :]).then_inc(s_gtr, 1)
                        pe.wait_ge(s_gcols, n + 1)
                        T.matmul(bank(1)[:, 0:HID], g_cols[:, :], we_f[:, :], start=True, stop=True).then_inc(s_gterm, 1)
                        pe.wait_ge(s_gmsg, n + 1)
                        apart(pe)
                        with pe.Fori(0, WINDOWS) as w:
                            pe.wait_ge(s_ghot, n * WINDOWS + w + 1)
                            T.matmul(p_win[0][:, 0:WIN], g_msg, g_hot, start=True, stop=True).then_inc(s_gwin, 1)
                    pe.wait_ge(s_gadd, (l + 1) * (EC * WINDOWS))
                    apart(pe)

                def hidden(c):
                    T.matmul(p_hid[:, 0:GA], w_now[:, 0:HID], z_cols[:, c * GN:c * GN + GA], start=True, stop=True)
                    T.matmul(p_hid[:, 512:512 + GB], w_now[:, 0:HID], z_cols[:, c * GN + GA:(c + 1) * GN],
                             start=True, stop=True).then_inc(s_hidp, 1)

                def new_h(c):
                    pe.wait_ge(s_h, l * GROUPS + c + 1)
                    pe.wait_ge(s_zc, (l + 1) * GROUPS + c)
                    transpose_h(h_rows[:, c, :])

                pe.wait_ge(s_added, (l + 1) * CHUNKS + 2)
                pe.wait_ge(s_wnow, l + 1)
                n = l * GROUPS
                hidden(0)
                for c in range(GROUPS):
                    pe.wait_ge(s_hid, n + c + 1)
                    if c >= 2:
                        pe.wait_ge(s_norm, n + c - 1)
                    apart(pe)
                    z = p_z2[c % 2][0:NB, :]
                    for b in range(BPG):
                        T.matmul(z[:, b * HID:(b + 1) * HID], ones_b[:, :], b2_parts[:, bass.ds(l * HID, HID)], start=True, stop=False)
                        last = T.matmul(z[:, b * HID:(b + 1) * HID], hid[:, b * NB:(b + 1) * NB], w_now[:, HID:2 * HID],
                                        start=False, stop=True)
                    last.then_inc(s_z2p, 1)
                    if c + 1 < GROUPS:
                        hidden(c + 1)
                    if c >= 2:
                        new_h(c - 2)
                for c in range(GROUPS - 2, GROUPS):
                    new_h(c)
                with pe.If(l < LAYERS - 1):
                    base, use = (l + 1) * CHUNKS, l * PAIRS
                    pe.wait_ge(s_str[0], (use + 1) * 32)
                    apart(pe)
                    for b in range(AHEAD):
                        sums(b, 0, (l + 1) * GROUPS)
                    edge_chunk(0, base, (l + 1) * GROUPS, (use + 1) * 32)
                    edge_chunk(1, base + 1, None, (use + 2) * 32)
                    with pe.Fori(1, PAIRS - 1) as i:
                        edge_chunk(0, base + i * 2, None, (use + i + 1) * 32)
                        edge_chunk(1, base + i * 2 + 1, None, (use + i + 2) * 32)
                    edge_chunk(0, base + CHUNKS - 2, None, (use + PAIRS) * 32)
                    edge_chunk(1, base + CHUNKS - 1)


_INS = ["x", "src", "dst", "edge_attr_16", "L0_gnn_We", "L0_gnn_be", "L0_gnn_W1", "L0_gnn_b1", "L0_gnn_W2", "L0_gnn_b2",
        "L0_gnn_ln_g", "L0_gnn_ln_b"]


def kernel(**inputs):
    import numpy as _np
    import concourse.bacc as _bacc
    from concourse import mybir as _mybir
    from concourse.bass_utils import run_bass_kernel_spmd as _run

    nc = _bacc.Bacc("TRN2", target_bir_lowering=False, num_devices=1)
    arrays, args = {}, []
    for name in _INS:
        a = _np.ascontiguousarray(inputs[name])
        arrays[f"in_{name}"] = a
        args.append(nc.dram_tensor(f"in_{name}", a.shape, _mybir.dt.from_np(a.dtype), kind="ExternalInput").ap())
    args.append(nc.dram_tensor("out", (NODES, HID), F32, kind="ExternalOutput").ap())
    gnn_kernel(nc, *args)
    r = _run(nc, [arrays], core_ids=[0])
    return r.results[0]["out"]
```
